# Optimizing a Trainium2 kernel written in Bass

```python
import numpy as np
import jax
import jax.numpy as jnp

def _softmax(x, axis=-1):
    return jax.nn.softmax(x, axis=axis)

def _gelu(x):
    return jax.nn.gelu(x, approximate=True)

def _silu(x):
    return jax.nn.silu(x)

def _sigmoid(x):
    return jax.nn.sigmoid(x)

def _layernorm(x, axis=-1, eps=1e-05):
    m = jnp.mean(x, axis=axis, keepdims=True)
    v = jnp.var(x, axis=axis, keepdims=True)
    return (x - m) / jnp.sqrt(v + eps)

def _scatter_add(tgt, idx, src, axis=0):
    return tgt.at[idx].add(src)

def _segment_sum(src, seg, n):
    return jax.ops.segment_sum(src, seg, n)
kernel_name = 'mk_macaron_d1_jaxref_r8_c8e553'

def setup_inputs(seed: int=0):
    np.random.seed(seed)
    _w = jnp.asarray

    def _L0_attn_setup():
        import jax, jax.numpy as jnp
        import numpy as np
        N_EMBD = 128
        N_HEAD = 16
        HORIZON = 64
        HS = N_EMBD // N_HEAD
        BD = max(HS // 4, 16)

        def _windows(t, delta):
            B, nh, T, D = t.shape
            padded = jnp.pad(t, ((0, 0), (0, 0), (delta - 1, 0), (0, 0)))
            idx = jnp.arange(T)[:, None] + jnp.arange(delta)[None, :]
            return padded[:, :, idx]
        key = jax.random.key(seed)
        ks = jax.random.split(key, 12)
        s = 0.02
        B, T = (2, 128)
        return {'x': jax.random.normal(ks[0], (B, T, N_EMBD), jnp.float32), 'W_disp': jax.random.normal(ks[1], (N_EMBD, N_HEAD * BD), jnp.float32) * s, 'W_val': jax.random.normal(ks[2], (N_EMBD, N_EMBD), jnp.float32) * s, 'rel_pos_emb': jax.random.normal(ks[3], (HORIZON, BD), jnp.float32) * s, 'W_strain': jax.random.normal(ks[4], (BD, BD), jnp.float32) * s, 'W_pos': jax.random.normal(ks[5], (BD, BD), jnp.float32) * s, 'W_bond': jax.random.normal(ks[6], (BD, 1), jnp.float32) * s, 'W_dmg': jax.random.normal(ks[7], (BD, BD), jnp.float32) * s, 'b_dmg': jnp.zeros((BD,), jnp.float32), 'W_dmg_out': jax.random.normal(ks[8], (BD, 1), jnp.float32) * s, 'b_dmg_out': jnp.full((1,), -3.0, jnp.float32), 'W_cproj': jax.random.normal(ks[9], (N_EMBD, N_EMBD), jnp.float32) * s}
    _L0_attn_in = _L0_attn_setup()

    def _L0_ffn_setup():
        import jax, jax.numpy as jnp
        import numpy as np
        B, T, D, F, E = (2, 128, 128, 512, 8)
        EPS = 1e-06
        key = jax.random.key(seed)
        k = jax.random.split(key, 5)
        scale = 0.02
        return {'x': jax.random.normal(k[0], (B, T, D), dtype=jnp.float32), 'rms_w': jnp.ones((D,), dtype=jnp.float32), 'gate_w': jax.random.normal(k[1], (E, D), dtype=jnp.float32) * scale, 'W1': jax.random.normal(k[2], (E, D, F), dtype=jnp.float32) * scale, 'b1': jnp.zeros((E, F), dtype=jnp.float32), 'W2': jax.random.normal(k[3], (E, F, D), dtype=jnp.float32) * scale, 'b2': jnp.zeros((E, D), dtype=jnp.float32)}
    _L0_ffn_in = _L0_ffn_setup()
    _d = {'L0_attn_x': _L0_attn_in['x'], 'L0_attn_W_disp': _L0_attn_in['W_disp'], 'L0_attn_W_val': _L0_attn_in['W_val'], 'L0_attn_rel_pos_emb': _L0_attn_in['rel_pos_emb'], 'L0_attn_W_strain': _L0_attn_in['W_strain'], 'L0_attn_W_pos': _L0_attn_in['W_pos'], 'L0_attn_W_bond': _L0_attn_in['W_bond'], 'L0_attn_W_dmg': _L0_attn_in['W_dmg'], 'L0_attn_b_dmg': _L0_attn_in['b_dmg'], 'L0_attn_W_dmg_out': _L0_attn_in['W_dmg_out'], 'L0_attn_b_dmg_out': _L0_attn_in['b_dmg_out'], 'L0_attn_W_cproj': _L0_attn_in['W_cproj'], 'L0_ffn_rms_w': _L0_ffn_in['rms_w'], 'L0_ffn_gate_w': _L0_ffn_in['gate_w'], 'L0_ffn_W1': _L0_ffn_in['W1'], 'L0_ffn_b1': _L0_ffn_in['b1'], 'L0_ffn_W2': _L0_ffn_in['W2'], 'L0_ffn_b2': _L0_ffn_in['b2']}
    _x0 = _d['L0_attn_x']
    _d['L0_attn_x'] = jax.random.normal(jax.random.fold_in(jax.random.key(seed), 1), (4, 1024, 128), dtype=_x0.dtype)
    del _x0
    return _d

def reference(L0_attn_x, L0_attn_W_disp, L0_attn_W_val, L0_attn_rel_pos_emb, L0_attn_W_strain, L0_attn_W_pos, L0_attn_W_bond, L0_attn_W_dmg, L0_attn_b_dmg, L0_attn_W_dmg_out, L0_attn_b_dmg_out, L0_attn_W_cproj, L0_ffn_rms_w, L0_ffn_gate_w, L0_ffn_W1, L0_ffn_b1, L0_ffn_W2, L0_ffn_b2):

    def _L0_attn_ref(x, W_disp, W_val, rel_pos_emb, W_strain, W_pos, W_bond, W_dmg, b_dmg, W_dmg_out, b_dmg_out, W_cproj):
        import jax, jax.numpy as jnp
        import numpy as np
        N_EMBD = 128
        N_HEAD = 16
        HORIZON = 64
        HS = N_EMBD // N_HEAD
        BD = max(HS // 4, 16)

        def _windows(t, delta):
            B, nh, T, D = t.shape
            padded = jnp.pad(t, ((0, 0), (0, 0), (delta - 1, 0), (0, 0)))
            idx = jnp.arange(T)[:, None] + jnp.arange(delta)[None, :]
            return padded[:, :, idx]
        B, T, C = x.shape
        nh, bd, hs = (N_HEAD, BD, HS)
        delta = min(HORIZON, T)
        disp = (x @ W_disp).reshape(B, T, nh, bd).transpose(0, 2, 1, 3)
        val = (x @ W_val).reshape(B, T, nh, hs).transpose(0, 2, 1, 3)
        disp_win = _windows(disp, delta)
        val_win = _windows(val, delta)
        cmask = jnp.arange(T)[:, None] - delta + 1 + jnp.arange(delta)[None, :] >= 0
        strain = disp_win - disp[:, :, :, None, :]
        rel_emb = rel_pos_emb[:delta]
        bond_act = jax.nn.gelu(strain @ W_strain + rel_emb @ W_pos, approximate=False)
        bond_logits = (bond_act @ W_bond)[..., 0]
        damage_act = jax.nn.gelu(strain @ W_dmg + b_dmg, approximate=False)
        damage = jax.nn.sigmoid((damage_act @ W_dmg_out)[..., 0] + b_dmg_out[0])
        logits = bond_logits - 10.0 * damage
        logits = jnp.where(cmask[None, None], logits, -jnp.inf)
        weights = jax.nn.softmax(logits, axis=-1)
        out = jnp.einsum('bntd,bntde->bnte', weights, val_win)
        out = out.transpose(0, 2, 1, 3).reshape(B, T, C)
        return out @ W_cproj

    def _L0_ffn_ref(x, rms_w, gate_w, W1, b1, W2, b2):
        import jax, jax.numpy as jnp
        import numpy as np
        B, T, D, F, E = (2, 128, 128, 512, 8)
        EPS = 1e-06
        ms = jnp.mean(x * x, axis=-1, keepdims=True)
        xn = x * jax.lax.rsqrt(ms + EPS) * rms_w
        logits = jnp.einsum('btd,ed->bte', xn, gate_w)
        scores = jax.nn.softmax(logits, axis=-1)
        top1_idx = jnp.argmax(scores, axis=-1)
        top1_score = jnp.max(scores, axis=-1)
        out = jnp.zeros_like(xn)
        for e in range(E):
            h = jax.nn.silu(jnp.einsum('btd,df->btf', xn, W1[e]) + b1[e])
            ye = jnp.einsum('btf,fd->btd', h, W2[e]) + b2[e]
            out = jnp.where((top1_idx == e)[..., None], ye, out)
        return out * top1_score[..., None]
    x = L0_attn_x
    x = x + 0.5 * _L0_ffn_ref(_layernorm(x, axis=-1), L0_ffn_rms_w, L0_ffn_gate_w, L0_ffn_W1, L0_ffn_b1, L0_ffn_W2, L0_ffn_b2)
    x = x + _L0_attn_ref(_layernorm(x, axis=-1), L0_attn_W_disp, L0_attn_W_val, L0_attn_rel_pos_emb, L0_attn_W_strain, L0_attn_W_pos, L0_attn_W_bond, L0_attn_W_dmg, L0_attn_b_dmg, L0_attn_W_dmg_out, L0_attn_b_dmg_out, L0_attn_W_cproj)
    x = x + 0.5 * _L0_ffn_ref(_layernorm(x, axis=-1), L0_ffn_rms_w, L0_ffn_gate_w, L0_ffn_W1, L0_ffn_b1, L0_ffn_W2, L0_ffn_b2)
    return x

_drawn_inputs = setup_inputs


def setup_inputs(seed=0):
    import zlib

    import numpy as np

    out = dict(_drawn_inputs(seed))
    spreads = {'L0_attn_b_dmg': (0.0, 0.8),
     'L0_ffn_rms_w': (1.0, 0.6),
     'L0_ffn_b1': (0.0, 0.8),
     'L0_ffn_b2': (0.0, 0.457)}
    factors = {'L0_attn_W_disp': 8.0,
     'L0_attn_W_val': 7.986,
     'L0_attn_rel_pos_emb': 8.0,
     'L0_attn_W_strain': 8.0,
     'L0_attn_W_pos': 8.0,
     'L0_attn_W_bond': 8.0,
     'L0_attn_W_dmg': 8.0,
     'L0_attn_W_dmg_out': 8.0,
     'L0_attn_W_cproj': 7.994,
     'L0_ffn_gate_w': 2.997,
     'L0_ffn_W1': 5.879,
     'L0_ffn_W2': 5.421}
    for name, (base, spread) in spreads.items():
        noise = np.random.default_rng([zlib.crc32(name.encode()), seed]).standard_normal(out[name].shape)
        drawn = base * np.exp(spread * noise) if base else spread * noise
        out[name] = jnp.asarray(drawn.astype(out[name].dtype))
    for name, factor in factors.items():
        out[name] = (out[name] * factor).astype(out[name].dtype)
    return out
```

```python
import concourse.bass as bass
from concourse import mybir
from contextlib import ExitStack


def prog(nc, x, W_disp, W_val, rel_pos_emb, W_strain, W_pos, W_bond, W_dmg, b_dmg, W_dmg_out,
         b_dmg_out, W_cproj, rms_w, gate_w, W1, b1, W2, b2, out):
    fp32 = mybir.dt.float32
    i32 = mybir.dt.int32
    ALU = mybir.AluOpType
    ACT = mybir.ActivationFunctionType
    AX = mybir.AxisListType

    B, T, D = x.shape
    HORIZON, BD = rel_pos_emb.shape
    H = W_disp.shape[1] // BD
    HS = D // H
    P = 128
    TILES = B * T // P
    TB = T // P
    HH = P // BD
    HALVES = H // HH
    BANK = 512
    NB = T // BANK
    OFFS = 16
    GROUPS = HORIZON // OFFS
    PAD = HORIZON
    VPAD = OFFS * (GROUPS - 1)
    VW = VPAD + T
    VROW = PAD + T
    LN_EPS = 1e-5
    RMS_EPS = 1e-6
    E, _, FF = W1.shape
    FC = FF // P
    NT = BANK // P

    PAIRS = OFFS // 2
    STEPS = 2 * GROUPS * PAIRS // 2
    RING = 4
    POOL_SLOTS = (3, 7)
    PA = GROUPS * len(POOL_SLOTS)
    DA_DMG = GROUPS * (PAIRS - len(POOL_SLOTS))
    DA = DA_DMG + GROUPS * PAIRS

    ctx = ExitStack()
    with ctx:
        def sb(name, shape, dt=fp32):
            return ctx.enter_context(nc.sbuf_tensor(name, shape, dt))

        def pb(name, cols):
            return ctx.enter_context(nc.psum_tensor(name, [P, cols], fp32))

        def sem(name):
            return ctx.enter_context(nc.semaphore(name))

        def window(first, dims):
            return bass.AP(tensor=first.tensor, offset=first.offset, ap=[first.ap[0]] + dims)

        X = sb("X", [P, TILES, D])
        YT = sb("YT", [P, B * T])
        A = [sb(f"A{i}", [P, 2, T]) for i in range(RING)]
        DPAD = sb("DPAD", [P, PAD + T])
        SPAD = sb("SPAD", [P, PAD + T])
        LT = [sb(f"LT{i}", [P, GROUPS, T]) for i in range(HALVES)]
        Y = [sb(f"Y{i}", [P, GROUPS, BANK]) for i in range(2)]
        RD = sb("RD", [P, T])
        O = sb("O", [P, T])
        M8 = sb("M8", [P, TB, HH])
        MREP = sb("MREP", [P, TB, OFFS, HH])
        LND = sb("LND", [P, TB, D])
        LNS = sb("LNS", [P, TB, D])
        STAT = sb("STAT", [P, 4, TB])
        NEGHALF = sb("NEGHALF", [P, TB])
        VS = sb("VS", [P, T])
        WFF = sb("WFF", [P, HS * VW])
        VSH = WFF[:, :].rearrange("p (e w) -> p e w", e=HS)
        W1S = WFF[:, 0:E * FF].rearrange("p (e f) -> p e f", e=E)
        W2S = WFF[:, E * FF:2 * E * FF].rearrange("p (e c d) -> p e c d", e=E, c=FC)
        HID = [A[i][:, :, :].rearrange("p a t -> p (a t)").rearrange("p (c t) -> p c t", c=FC)
               for i in range(2)]
        XT = YT[:, 0:T]
        ROWS = sb("ROWS", [E * FC + E + 1, D])
        COLS = sb("COLS", [P, E * FC + E + 1])
        B2R = sb("B2R", [1, E, D])
        ONES = sb("ONES", [1, P])
        GATE = sb("GATE", [P, 4, TB, E])
        GSUM = sb("GSUM", [P, 3, TB])
        IT = sb("IT", [P, 4], i32)
        ITF = sb("ITF", [P, 4])
        COLI = sb("COLI", [P, 128], i32)
        COL = sb("COL", [P, 128])
        COLH = sb("COLH", [P, 128])
        COLBI = sb("COLBI", [P, 128], i32)
        COLB = sb("COLB", [P, 128])
        COLHI = sb("COLHI", [P, 128], i32)
        CMI = sb("CMI", [P, GROUPS, PAD], i32)
        CMASK = sb("CMASK", [P, GROUPS, PAD])
        IDENT = sb("IDENT", [P, P])
        SELALL = sb("SELALL", [P, P])
        SELE = sb("SELE", [P, 2, 32])
        WSEL = sb("WSEL", [P, 2, 4, 32])
        WCOL = sb("WCOL", [P, 2])
        BDMG = sb("BDMG", [P, 1])
        BOUT = sb("BOUT", [P, 1])
        BOUTH = sb("BOUTH", [P, 1])
        WREP = sb("WREP", [P, 2, BD])
        BDW = sb("BDW", [P, 2, P])
        REL = sb("REL", [HORIZON, BD])
        RELT = sb("RELT", [BD, HORIZON])
        WPOS = sb("WPOS", [BD, BD])
        WPOSR = sb("WPOSR", [BD, HH, BD])
        PCOL = sb("PCOL", [P, HORIZON])
        WDISP = sb("WDISP", [P, HALVES * P])
        WDT = sb("WDT", [P, HALVES, P])
        F = sb("F", [P, HALVES, 2, P])
        WVAL = sb("WVAL", [P, D])
        WC = sb("WC", [P, HALVES, D])
        ZP = sb("ZP", [P, PAD])

        CT = pb("CT", T)
        ACC = [pb("ACC0", T), pb("ACC1", T)]
        MX = [pb("MX0", BANK), pb("MX1", BANK)]

        vd = nc.dram_tensor("values_scratch", (B, D, VROW), fp32, kind="Internal").ap()

        x_loaded = sem("x_loaded")
        ffn_loaded = sem("ffn_loaded")
        cols_ready = sem("cols_ready")
        fv = sem("ffn_norm_vector")
        fa = sem("ffn_norm_scalar")
        fg = sem("ffn_norm_pool")
        fp = sem("ffn_transposed")
        xt_ready = sem("xt_ready")
        gate_logits = sem("gate_logits")
        gate_steps = sem("gate_steps")
        gate_exp = sem("gate_exp")
        up_done = sem("up_done")
        silu_done = sem("silu_done")
        down_done = sem("down_done")
        y_added = sem("y_added")
        gate_ready = sem("gate_ready")
        w_loaded = sem("w_loaded")
        pool_const = sem("pool_const")
        dve_const = sem("dve_const")
        pe_const = sem("pe_const")
        consts_ready = sem("consts_ready")
        weights_ready = sem("weights_ready")
        yt_ready = sem("yt_ready")
        ln_v = sem("ln_v")
        ln_a = sem("ln_a")
        ln_g = sem("ln_g")
        ln_p = sem("ln_p")
        val_done = sem("val_done")
        val_copied = sem("val_copied")
        val_stored = sem("val_stored")
        ct_ready = sem("ct_ready")
        pad_ready = sem("pad_ready")
        dve_args = sem("dve_args")
        pool_args = sem("pool_args")
        gelu_done = sem("gelu_done")
        pe_used = sem("pe_used")
        tanh_done = sem("tanh_done")
        bond_evac = sem("bond_evac")
        masked = sem("masked")
        transposed = sem("transposed")
        max_done = sem("max_done")
        mrep_done = sem("mrep_done")
        mbc_done = sem("mbc_done")
        shifted = sem("shifted")
        exp_done = sem("exp_done")
        den_done = sem("den_done")
        recip_done = sem("recip_done")
        vsh_loaded = sem("vsh_loaded")
        prod_done = sem("prod_done")
        num_used = sem("num_used")
        norm_done = sem("norm_done")
        cproj_done = sem("cproj_done")
        x_added = sem("x_added")
        out_stored = sem("out_stored")

        def up_bank(f):
            return (CT, ACC[1])[f // 2][:, (f % 2) * BANK:(f % 2 + 1) * BANK]

        block = ctx.enter_context(nc.Block())

        WL = 16 * (4 + 1 + 8 + 8 + 8 + 8 + 8 + 1 + 1 + 1 + 1 + 16 + 1)

        @block.sync
        def _(sp):
            for b in range(B):
                sp.dma_start(X[:, b * TB:(b + 1) * TB, :],
                             x[b].rearrange("(n p) d -> p n d", p=P)).then_inc(x_loaded, 16)
            sp.dma_start(ROWS[0:E * FC, :], b1.rearrange("e (c f) -> (e c) f", c=FC)).then_inc(w_loaded, 16)
            sp.dma_start(ROWS[E * FC:E * FC + E, :], gate_w).then_inc(w_loaded, 16)
            sp.dma_start(ROWS[E * FC + E:E * FC + E + 1, :], rms_w.unsqueeze(0)).then_inc(w_loaded, 16)
            sp.dma_start(B2R[:, :, :], b2.unsqueeze(0)).then_inc(w_loaded, 16)

            def load_experts():
                sp.dma_start(W1S, W1.rearrange("e d f -> d e f")).then_inc(ffn_loaded, 16)
                sp.dma_start(W2S, W2.rearrange("e (c f) d -> f (e c) d", c=FC).rearrange(
                    "f (e c) d -> f e c d", c=FC)).then_inc(ffn_loaded, 16)
            load_experts()
            sp.dma_start(WDISP[:, :], W_disp).then_inc(w_loaded, 16)
            for h in range(HH):
                rows = slice(h * BD, (h + 1) * BD)
                sp.dma_start(WREP[rows, 0, :], W_strain).then_inc(w_loaded, 16)
                sp.dma_start(WREP[rows, 1, :], W_dmg).then_inc(w_loaded, 16)
                sp.dma_start(WCOL[rows, 0:1], W_bond).then_inc(w_loaded, 16)
                sp.dma_start(WCOL[rows, 1:2], W_dmg_out).then_inc(w_loaded, 16)
                sp.dma_start(BDMG[rows, :], b_dmg.unsqueeze(1)).then_inc(w_loaded, 16)
            sp.dma_start(REL[:, :], rel_pos_emb).then_inc(w_loaded, 16)
            sp.dma_start(WPOS[:, :], W_pos).then_inc(w_loaded, 16)
            sp.dma_start(WVAL[:, :], W_val).then_inc(w_loaded, 16)
            sp.dma_start(BOUT[:, :], b_dmg_out.partition_broadcast(P)).then_inc(w_loaded, 16)
            sp.wait_ge(dve_const, 1)
            for hh in range(HALVES):
                for e in range(HS):
                    row = 32 * (e // 2) + 8 * (e % 2)
                    sp.dma_start(WC[row:row + HH, hh, :],
                                 W_cproj.rearrange("(h e) d -> e h d", e=HS)[e, hh * HH:(hh + 1) * HH, :]
                                 ).then_inc(w_loaded, 16)
            sp.wait_ge(dve_const, 2)
            sp.dma_start(vd[:, :, 0:PAD].rearrange("b c w -> c b w"),
                         ZP[:, :].unsqueeze(1).broadcast_to([P, B, PAD])).then_inc(w_loaded, 16)

            def store_values(b):
                sp.wait_ge(val_copied, b + 1)
                sp.dma_start(vd[b, :, PAD:VROW], VS[:, :]).then_inc(val_stored, 16)
            for b in range(B):
                store_values(b)
            sp.wait_ge(val_stored, 16 * B)
            sp.wait_ge(w_loaded, WL)

            def load_values(b, hh, u):
                if isinstance(u, int) and u == 0:
                    sp.wait_ge(y_added, B * 2 * E)
                else:
                    sp.wait_ge(prod_done, 16 * u)
                for j in range(OFFS):
                    row = 32 * (j % 4) + 8 * (j // 4)
                    first = PAD - VPAD - j
                    src = vd[b, hh * HH * HS:(hh + 1) * HH * HS, first:first + VW]
                    sp.dma_start(VSH[row:row + HH, :, :], src.rearrange("(h e) w -> h e w", e=HS)
                                 ).then_inc(vsh_loaded, 16)

            def store(b):
                sp.wait_ge(y_added, (B + b + 1) * 2 * E)
                sp.dma_start(out[b].rearrange("(n p) d -> p n d", p=P),
                             X[:, b * TB:(b + 1) * TB, :]).then_inc(out_stored, 16)
            for hh in range(HALVES):
                load_values(0, hh, hh)
            with sp.Fori(1, B) as b:
                for hh in range(HALVES):
                    load_values(b, hh, 2 * b + hh)
            sp.wait_ge(prod_done, 16 * 2 * B)
            load_experts()
            for b in range(B):
                store(b)
            sp.wait_ge(out_stored, 16 * B)

        @block.gpsimd
        def _(pool):
            pool.iota(IT[:, 0:1], [[0, 1]], base=0, channel_multiplier=1).then_inc(pool_const, 1)
            pool.iota(COLI[:, :], [[1, 128]], base=0, channel_multiplier=0).then_inc(pool_const, 1)
            pool.iota(COLHI[:, :], [[0, 16], [1, 8]], base=0, channel_multiplier=0).then_inc(pool_const, 1)
            pool.iota(COLBI[:, :], [[1, 8], [0, 16]], base=0, channel_multiplier=0).then_inc(pool_const, 1)
            pool.iota(CMI[:, :, :], [[-OFFS, GROUPS], [1, PAD]], base=0, channel_multiplier=0
                      ).then_inc(pool_const, 1)
            pool.memset(NEGHALF[:, :], -0.5).then_inc(pool_const, 1)
            pool.wait_ge(pool_const, 6)

            def ffn_norm(b):
                for i in range(2):
                    pool.wait_ge(fv, 9 * b + 5 + 3 * i)
                    pool.tensor_tensor(STAT[:, 3, :], STAT[:, 2, :], NEGHALF[:, :], ALU.pow).then_inc(fg, 1)
            with pool.Fori(0, B) as b:
                ffn_norm(b)
            for b in range(B):
                pool.wait_ge(ln_v, 6 * b + 5)
                pool.tensor_tensor(STAT[:, 3, :], STAT[:, 2, :], NEGHALF[:, :], ALU.pow).then_inc(ln_g, 1)

            def difference(u, g, p):
                n = 8 * g + p
                pool.wait_ge(pad_ready, 2 * u + 1)
                if not (isinstance(u, int) and u == 0 and n < RING):
                    pool.wait_ge(pe_used, 32 * u + (n - RING) // 2 + 1)
                j = OFFS * g + 2 * p
                pool.tensor_tensor(A[n % RING][:, :, :], window(DPAD[:, PAD - j - 1:PAD - j], [[1, 2], [1, T]]),
                                   window(DPAD[:, PAD:PAD + 1], [[0, 2], [1, T]]), ALU.subtract).then_inc(pool_args, 1)

            def product(v, hh, i):
                half, e = divmod(i, HS)
                first = VPAD + half * BANK
                if i == 0:
                    pool.wait_ge(exp_done, v + 1)
                    pool.wait_ge(vsh_loaded, 16 * OFFS * (v + 1))
                if not (isinstance(v, int) and v == 0 and i < 2):
                    pool.wait_ge(num_used, 16 * v + i - 1)
                pool.tensor_tensor(Y[i % 2][:, :, :], LT[hh][:, :, half * BANK:(half + 1) * BANK],
                                   window(VSH[:, e, first:first + 1], [[-OFFS, GROUPS], [1, BANK]]),
                                   ALU.mult).then_inc(prod_done, 1)

            def unit(u, hh, v):
                for g in range(GROUPS):
                    for k, p in enumerate(POOL_SLOTS):
                        if v is not None and 2 * g + k >= 2 * GROUPS - 2:
                            product(v, 1 - hh, 2 * g + k - (2 * GROUPS - 2))
                        difference(u, g, p)
                if v is not None:
                    for i in range(2, 2 * HS):
                        product(v, 1 - hh, i)
            unit(0, 0, None)
            unit(1, 1, 0)
            with pool.Fori(1, B) as b:
                for hh in range(HALVES):
                    unit(2 * b + hh, hh, 2 * b + hh - 1)
            for i in range(2 * HS):
                product(2 * B - 1, 1, i)
            with pool.Fori(B, 2 * B) as b:
                ffn_norm(b)

        @block.scalar
        def _(act):
            def ffn(r):
                act.wait_ge(fv, 9 * r + 3)
                act.activation(LNS[:, :, :], LND[:, :, :], ACT.Square).then_inc(fa, 1)
                act.wait_ge(fv, 9 * r + 6)
                act.activation(LNS[:, :, :], LND[:, :, :], ACT.Square).then_inc(fa, 1)
                act.wait_ge(gate_steps, 6 * r + 2)
                act.activation(GATE[:, 1, :, :], GATE[:, 0, :, :], ACT.Exp).then_inc(gate_exp, 1)
                for i in range(2 * E):
                    w = 2 * E * r + i
                    for f in range(FC):
                        act.wait_ge(up_done, FC * w + f + 1)
                        if not (isinstance(r, int) and r == 0 and i < 2):
                            act.wait_ge(down_done, w - 1)
                        k = FC * (i % E) + f
                        act.activation(HID[i % 2][:, f, :], up_bank(f), ACT.Silu, bias=COLS[:, k:k + 1]
                                       ).then_inc(silu_done, 1)
            act.wait_ge(cols_ready, 1)
            act.wait_ge(dve_const, 3)
            ffn(0)
            with act.Fori(1, B) as b:
                ffn(b)
            for b in range(B):
                act.wait_ge(ln_v, 6 * b + 3)
                act.activation(LNS[:, :, :], LND[:, :, :], ACT.Square).then_inc(ln_a, 1)
                act.wait_ge(val_done, b + 1)
                if b > 0:
                    act.wait_ge(val_stored, 16 * b)
                act.activation(VS[:, :], CT[:, :], ACT.Copy).then_inc(val_copied, 1)

            def gelu(u, g, p):
                n = 8 * g + p
                if g < GROUPS:
                    mine = sum(1 for s in POOL_SLOTS if s < p)
                    if p in POOL_SLOTS:
                        act.wait_ge(pool_args, PA * u + len(POOL_SLOTS) * g + mine + 1)
                    else:
                        act.wait_ge(dve_args, DA * u + (PAIRS - len(POOL_SLOTS)) * g + p - mine + 1)
                    bias = BDMG[:, :]
                else:
                    act.wait_ge(dve_args, DA * u + DA_DMG + n - PAIRS * GROUPS + 1)
                    bias = 0.0
                act.activation(A[n % RING][:, :, :], A[n % RING][:, :, :], ACT.Gelu, bias=bias
                               ).then_inc(gelu_done, 1)

            def damage(u, hh, g):
                act.wait_ge(pe_used, 4 * (8 * u + g + 1))
                act.activation(LT[hh][:, g, :], ACC[g % 2][:, :], ACT.Tanh, bias=BOUTH[:, :], scale=0.5
                               ).then_inc(tanh_done, 1)

            def exponentials(v, hh):
                act.wait_ge(shifted, 2 * v + 2)
                act.activation(LT[hh][:, :, :], LT[hh][:, :, :], ACT.Exp).then_inc(exp_done, 1)

            def unit(u, hh, v):
                for g in range(2 * GROUPS):
                    for p in range(PAIRS):
                        if v is not None and 8 * g + p == 20:
                            exponentials(v, 1 - hh)
                        if 1 <= g <= GROUPS and p == 4:
                            damage(u, hh, g - 1)
                        gelu(u, g, p)
            unit(0, 0, None)
            unit(1, 1, 0)
            with act.Fori(1, B) as b:
                for hh in range(HALVES):
                    unit(2 * b + hh, hh, 2 * b + hh - 1)
            exponentials(2 * B - 1, 1)
            with act.Fori(B, 2 * B) as r:
                ffn(r)

        @block.vector
        def _(dve):
            dve.memset(WC[:, :, :], 0.0).then_inc(dve_const, 1)
            dve.memset(ZP[:, :], 0.0).then_inc(dve_const, 1)
            dve.wait_ge(w_loaded, WL)
            dve.tensor_scalar(BOUTH[:, :], BOUT[:, :], 0.5, None, ALU.mult).then_inc(dve_const, 1)
            done = [3]

            def step(ins):
                ins.then_inc(dve_const, 1)
                done[0] += 1
                dve.wait_ge(dve_const, done[0])
            step(dve.memset(DPAD[:, 0:PAD], 0.0))
            step(dve.memset(SPAD[:, 0:PAD], 0.0))
            step(dve.memset(ONES[:, :], 1.0))
            dve.wait_ge(pool_const, 6)
            step(dve.tensor_scalar(IT[:, 1:2], IT[:, 0:1], 5, None, ALU.logical_shift_right))
            step(dve.tensor_scalar(IT[:, 2:3], IT[:, 0:1], 3, 3, ALU.logical_shift_right, ALU.bitwise_and))
            step(dve.tensor_scalar(ITF[:, 0:1], IT[:, 2:3], 4.0, None, ALU.mult))
            step(dve.tensor_copy(ITF[:, 1:2], IT[:, 1:2]))
            step(dve.tensor_tensor(ITF[:, 0:1], ITF[:, 0:1], ITF[:, 1:2], ALU.add))
            step(dve.tensor_scalar(IT[:, 3:4], IT[:, 0:1], 7, None, ALU.bitwise_and))
            step(dve.tensor_copy(ITF[:, 1:2], IT[:, 3:4]))
            step(dve.tensor_scalar(IT[:, 3:4], IT[:, 0:1], 4, None, ALU.logical_shift_right))
            step(dve.tensor_copy(ITF[:, 2:3], IT[:, 3:4]))
            step(dve.tensor_copy(ITF[:, 3:4], IT[:, 0:1]))
            step(dve.tensor_copy(COL[:, :], COLI[:, :]))
            step(dve.tensor_copy(COLH[:, :], COLHI[:, :]))
            step(dve.tensor_copy(COLB[:, :], COLBI[:, :]))
            step(dve.tensor_copy(CMASK[:, :, :], CMI[:, :, :]))
            step(dve.tensor_scalar(CMASK[:, :, :], CMASK[:, :, :], ITF[:, 0:1], -1e30, ALU.is_lt, ALU.mult))
            step(dve.tensor_scalar(IDENT[:, :], COL[:, :], ITF[:, 3:4], None, ALU.is_equal))
            step(dve.tensor_scalar(SELALL[:, :], COLH[:, :], ITF[:, 1:2], None, ALU.is_equal))
            for par in range(2):
                step(dve.tensor_scalar(SELE[:, par, :], COL[:, 0:32], -8.0 * par, ITF[:, 1:2], ALU.add,
                                       ALU.is_equal))
            for kind in range(2):
                for k in range(4):
                    step(dve.tensor_scalar(WSEL[:, kind, k, :], COL[:, 0:32], -8.0 * k, ITF[:, 2:3],
                                           ALU.add, ALU.is_equal))
                    step(dve.tensor_scalar(WSEL[:, kind, k, :], WSEL[:, kind, k, :], WCOL[:, kind:kind + 1],
                                           None, ALU.mult))
            step(dve.tensor_scalar(COLB[:, :], COLB[:, :], ITF[:, 2:3], None, ALU.is_equal))
            for kind in range(2):
                step(dve.tensor_tensor(BDW[:, kind, :].rearrange("p (h c) -> p h c", c=BD),
                                       COLB[:, :].rearrange("p (h c) -> p h c", c=BD),
                                       WREP[:, kind, :].unsqueeze(1).broadcast_to([P, HH, BD]), ALU.mult))
            dve.tensor_copy(WPOSR[:, :, :], WPOS[:, :].unsqueeze(1).broadcast_to([BD, HH, BD])
                            ).then_inc(consts_ready, 1)
            dve.wait_ge(pe_const, 1)
            dve.tensor_copy(RELT[:, :], MX[0][0:BD, 0:HORIZON]).then_inc(weights_ready, 1)
            dve.wait_ge(pe_const, 2)
            dve.tensor_copy(WDT[:, :, :].rearrange("p h c -> p (h c)"), MX[1][:, 0:HALVES * P]).then_inc(weights_ready, 1)
            dve.wait_ge(pe_const, 3)
            dve.tensor_copy(PCOL[:, :], MX[0][:, 0:HORIZON]).then_inc(weights_ready, 1)
            dve.wait_ge(pe_const, 4)
            dve.tensor_copy(F[:, :, :, :].rearrange("p h k c -> p (h k c)"), MX[1][:, :]).then_inc(weights_ready, 1)

            dve.wait_ge(pe_const, 5)
            dve.tensor_copy(COLS[:, :], MX[0][:, 0:E * FC + E + 1]).then_inc(cols_ready, 1)
            dve.wait_ge(cols_ready, 1)

            def ffn(r, b):
                first = isinstance(r, int) and r == 0
                xb = X[:, bass.ds(b * TB, TB), :]
                if not first:
                    dve.wait_ge(y_added, 2 * E * r)
                v0 = 9 * r
                dve.tensor_reduce(STAT[:, 0, :], xb, AX.X, ALU.add).then_inc(fv, 1)
                dve.wait_ge(fv, v0 + 1)
                dve.tensor_scalar(STAT[:, 1, :], STAT[:, 0, :], 1.0 / D, None, ALU.mult).then_inc(fv, 1)
                dve.wait_ge(fv, v0 + 2)
                dve.tensor_tensor(LND[:, :, :], xb, STAT[:, 1, :].unsqueeze(2).broadcast_to([P, TB, D]),
                                  ALU.subtract).then_inc(fv, 1)
                for i in range(2):
                    dve.wait_ge(fa, 2 * r + i + 1)
                    dve.tensor_reduce(STAT[:, 0, :], LNS[:, :, :], AX.X, ALU.add).then_inc(fv, 1)
                    dve.wait_ge(fv, v0 + 4 + 3 * i)
                    dve.tensor_scalar(STAT[:, 2, :], STAT[:, 0, :], 1.0 / D, (LN_EPS, RMS_EPS)[i], ALU.mult,
                                      ALU.add).then_inc(fv, 1)
                    dve.wait_ge(fg, 2 * r + i + 1)
                    dve.tensor_tensor(LND[:, :, :], LND[:, :, :],
                                      STAT[:, 3, :].unsqueeze(2).broadcast_to([P, TB, D]), ALU.mult
                                      ).then_inc(fv, 1)
                dve.wait_ge(fp, r + 1)
                dve.tensor_scalar(XT, ACC[0][:, :], COLS[:, E * FC + E:E * FC + E + 1], None, ALU.mult
                                  ).then_inc(xt_ready, 1)
                dve.wait_ge(gate_logits, r + 1)
                lg = MX[0][:, 0:TB * E].rearrange("p (n e) -> p n e", e=E)
                g0 = 6 * r
                dve.tensor_reduce(GSUM[:, 0, :], lg, AX.X, ALU.max).then_inc(gate_steps, 1)
                dve.wait_ge(gate_steps, g0 + 1)
                dve.tensor_tensor(GATE[:, 0, :, :], lg, GSUM[:, 0, :].unsqueeze(2).broadcast_to([P, TB, E]),
                                  ALU.subtract).then_inc(gate_steps, 1)
                dve.wait_ge(gate_steps, g0 + 2)
                dve.tensor_scalar(GATE[:, 2, :, :], GATE[:, 0, :, :], 0.0, -16.0, ALU.is_ge, ALU.mult
                                  ).then_inc(gate_steps, 1)
                dve.wait_ge(gate_steps, g0 + 3)
                dve.tensor_tensor(GATE[:, 2, :, :], GATE[:, 2, :, :],
                                  COL[:, 0:E].unsqueeze(1).broadcast_to([P, TB, E]), ALU.add
                                  ).then_inc(gate_steps, 1)
                dve.wait_ge(gate_steps, g0 + 4)
                dve.tensor_reduce(GSUM[:, 1, :], GATE[:, 2, :, :], AX.X, ALU.min)
                dve.wait_ge(gate_exp, r + 1)
                dve.tensor_reduce(GSUM[:, 2, :], GATE[:, 1, :, :], AX.X, ALU.add).then_inc(gate_steps, 1)
                dve.wait_ge(gate_steps, g0 + 5)
                dve.reciprocal(GSUM[:, 0, :], GSUM[:, 2, :])
                dve.tensor_tensor(GATE[:, 3, :, :], GATE[:, 2, :, :],
                                  GSUM[:, 1, :].unsqueeze(2).broadcast_to([P, TB, E]), ALU.is_equal
                                  ).then_inc(gate_steps, 1)
                dve.wait_ge(gate_steps, g0 + 6)
                dve.scalar_tensor_tensor(GATE[:, 2, :, :], GATE[:, 3, :, :], 0.5,
                                         GSUM[:, 0, :].unsqueeze(2).broadcast_to([P, TB, E]), ALU.mult, ALU.mult
                                         ).then_inc(gate_ready, 1)
                dve.wait_ge(gate_ready, r + 1)
                for i in range(2 * E):
                    w = 2 * E * r + i
                    c, e = divmod(i, E)
                    dve.wait_ge(down_done, w + 1)
                    if not (first and i == 0):
                        dve.wait_ge(y_added, w)
                    for n in range(NT):
                        tile = c * NT + n
                        xs = X[:, bass.ds(b * TB + tile, 1), :].rearrange("p n d -> p (n d)")
                        last = dve.scalar_tensor_tensor(xs, MX[i % 2][:, n * D:(n + 1) * D],
                                                        GATE[:, 2, tile, e:e + 1], xs, ALU.mult, ALU.add)
                    last.then_inc(y_added, 1)
            dve.wait_ge(x_loaded, 16 * B)
            ffn(0, 0)
            with dve.Fori(1, B) as b:
                ffn(b, b)
            dve.wait_ge(y_added, 2 * E * B)

            for b in range(B):
                xb = X[:, b * TB:(b + 1) * TB, :]
                dve.wait_ge(x_loaded, 16 * B)
                if b > 0:
                    dve.wait_ge(ln_a, b)
                    dve.wait_ge(ln_p, b)
                v0 = 6 * b
                dve.tensor_reduce(STAT[:, 0, :], xb, AX.X, ALU.add).then_inc(ln_v, 1)
                dve.wait_ge(ln_v, v0 + 1)
                dve.tensor_scalar(STAT[:, 1, :], STAT[:, 0, :], 1.0 / D, None, ALU.mult).then_inc(ln_v, 1)
                dve.wait_ge(ln_v, v0 + 2)
                dve.tensor_tensor(LND[:, :, :], xb, STAT[:, 1, :].unsqueeze(2).broadcast_to([P, TB, D]),
                                  ALU.subtract).then_inc(ln_v, 1)
                dve.wait_ge(ln_a, b + 1)
                dve.tensor_reduce(STAT[:, 0, :], LNS[:, :, :], AX.X, ALU.add).then_inc(ln_v, 1)
                dve.wait_ge(ln_v, v0 + 4)
                if b > 0:
                    dve.wait_ge(ln_g, b)
                dve.tensor_scalar(STAT[:, 2, :], STAT[:, 0, :], 1.0 / D, LN_EPS, ALU.mult, ALU.add
                                  ).then_inc(ln_v, 1)
                dve.wait_ge(ln_g, b + 1)
                dve.tensor_tensor(LND[:, :, :], LND[:, :, :],
                                  STAT[:, 3, :].unsqueeze(2).broadcast_to([P, TB, D]), ALU.mult
                                  ).then_inc(ln_v, 1)
                dve.wait_ge(ln_p, b + 1)
                dve.tensor_copy(YT[:, b * T:(b + 1) * T], ACC[0][:, :]).then_inc(yt_ready, 1)

            def copy_pad(u, kind):
                dve.wait_ge(ct_ready, 2 * u + kind + 1)
                if kind == 0 and not (isinstance(u, int) and u == 0):
                    dve.wait_ge(pool_args, PA * u)
                dve.tensor_copy((DPAD, SPAD)[kind][:, PAD:PAD + T], CT[:, :]).then_inc(pad_ready, 1)
                dve.wait_ge(pad_ready, 2 * u + kind + 1)

            def difference(u, g, p):
                n = 8 * g + p
                if not (isinstance(u, int) and u == 0 and n < RING):
                    dve.wait_ge(pe_used, 32 * u + (n - RING) // 2 + 1)
                slot = A[n % RING]
                j = OFFS * (g % GROUPS) + 2 * p
                if g < GROUPS:
                    dve.tensor_tensor(slot[:, :, :], window(DPAD[:, PAD - j - 1:PAD - j], [[1, 2], [1, T]]),
                                      window(CT[:, 0:1], [[0, 2], [1, T]]), ALU.subtract).then_inc(dve_args, 1)
                else:
                    for i in range(2):
                        ji = j + 1 - i
                        last = dve.scalar_tensor_tensor(
                            slot[:, i, :], SPAD[:, PAD - ji:PAD - ji + T],
                            PCOL[:, HORIZON - 1 - ji:HORIZON - ji], CT[:, :], ALU.add, ALU.subtract)
                    last.then_inc(dve_args, 1)

            def logits(u, hh, g):
                dve.wait_ge(pe_used, 4 * (8 * u + g + 1))
                dve.wait_ge(tanh_done, 4 * u + g - 3)
                lt = LT[hh][:, g - GROUPS, :]
                dve.scalar_tensor_tensor(lt, lt, -5.0, ACC[g % 2][:, :], ALU.mult, ALU.add
                                         ).then_inc(bond_evac, 1)

            def tail(v, vb, hh, s):
                lt = LT[hh]
                if s == 2:
                    logits(v, hh, 2 * GROUPS - 1)
                    dve.wait_ge(bond_evac, 4 * v + 4)
                    dve.tensor_tensor(lt[:, :, 0:PAD], lt[:, :, 0:PAD], CMASK[:, :, :], ALU.add
                                      ).then_inc(masked, 1)
                if 5 <= s <= 8:
                    for tb in (2 * (s - 5), 2 * (s - 5) + 1):
                        dve.wait_ge(transposed, TB * v + tb + 1)
                        dve.tensor_reduce(M8[:, tb, :], MX[tb % 2][:, :].rearrange("p (j h) -> p h j", h=HH),
                                          AX.X, ALU.max).then_inc(max_done, 1)
                if s == 8:
                    dve.wait_ge(max_done, TB * (v + 1))
                    for i in range(2):
                        blocks = slice(i * TB // 2, (i + 1) * TB // 2)
                        last = dve.tensor_copy(MREP[:, blocks, :, :],
                                               M8[:, blocks, :].unsqueeze(2).broadcast_to([P, TB // 2, OFFS, HH]))
                        last.then_inc(mrep_done, 1)
                if s == 10:
                    for half in range(2):
                        dve.wait_ge(mbc_done, 2 * v + half + 1)
                        cols = slice(half * BANK, (half + 1) * BANK)
                        dve.tensor_tensor(lt[:, :, cols], lt[:, :, cols],
                                          window(MX[half][:, 0:1], [[0, GROUPS], [1, BANK]]), ALU.subtract
                                          ).then_inc(shifted, 1)
                if s in (13, 14):
                    half = s - 13
                    dve.wait_ge(den_done, 2 * v + half + 1)
                    dve.reciprocal(RD[:, half * BANK:(half + 1) * BANK], MX[1][:, :]).then_inc(recip_done, 1)
                if s in (23, 31):
                    half = (s - 23) // 8
                    cols = slice(half * BANK, (half + 1) * BANK)
                    dve.wait_ge(num_used, 16 * v + 8 * (half + 1))
                    if half == 0:
                        dve.wait_ge(recip_done, 2 * v + 2)
                        if not (isinstance(v, int) and v == 0):
                            dve.wait_ge(cproj_done, 2 * v)
                    dve.tensor_tensor(O[:, cols], MX[0][:, :], RD[:, cols], ALU.mult).then_inc(norm_done, 1)
                if s in (26, 33):
                    half = (s - 26) // 7
                    dve.wait_ge(cproj_done, 2 * v + half + 1)
                    first = vb * TB + half * TB // 2
                    xs = X[:, bass.ds(first, TB // 2), :]
                    dve.tensor_tensor(xs, xs, MX[1][:, :].rearrange("p (n d) -> p n d", d=D), ALU.add
                                      ).then_inc(x_added, 1)

            def unit(u, hh, v, vb, v2, vb2):
                copy_pad(u, 0)
                for g in range(2 * GROUPS):
                    if g == GROUPS:
                        copy_pad(u, 1)
                    for p in range(PAIRS):
                        if not (g < GROUPS and p in POOL_SLOTS):
                            difference(u, g, p)
                        if GROUPS + 1 <= g and p == 4:
                            logits(u, hh, g - 1)
                        if p % 2 == 1:
                            s = 4 * g + p // 2
                            if s == 1 and v2 is not None:
                                tail(v2, vb2, hh, 33)
                            if v is not None:
                                tail(v, vb, 1 - hh, s)
            unit(0, 0, None, None, None, None)
            unit(1, 1, 0, 0, None, None)
            with dve.Fori(1, B) as b:
                unit(2 * b, 0, 2 * b - 1, b - 1, 2 * b - 2, b - 1)
                unit(2 * b + 1, 1, 2 * b, b, 2 * b - 1, b - 1)
            tail(2 * B - 2, B - 1, 0, 33)
            for s in range(34):
                tail(2 * B - 1, B - 1, 1, s)
            dve.wait_ge(x_added, 4 * B)
            with dve.Fori(0, B) as b:
                ffn(b + B, b)

        @block.tensor
        def _(pe):
            pe.wait_ge(consts_ready, 1)
            pe.wait_ge(w_loaded, WL)
            pe.transpose(MX[0][0:BD, 0:HORIZON], REL[:, :], IDENT[0:HORIZON, 0:HORIZON]).then_inc(pe_const, 1)
            for hh in range(HALVES):
                last = pe.transpose(MX[1][:, hh * P:(hh + 1) * P], WDISP[:, hh * P:(hh + 1) * P], IDENT[:, :])
            last.then_inc(pe_const, 1)
            pe.wait_ge(weights_ready, 2)
            pe.matmul(MX[0][:, 0:HORIZON], WPOSR[:, :, :].rearrange("p h c -> p (h c)"), RELT[:, :],
                      start=True, stop=True).then_inc(pe_const, 1)
            for hh in range(HALVES):
                for kind in range(2):
                    col = (2 * hh + kind) * P
                    last = pe.matmul(MX[1][:, col:col + P], WDT[:, hh, :], BDW[:, 1 - kind, :],
                                     start=True, stop=True)
            last.then_inc(pe_const, 1)
            n = E * FC + E + 1
            pe.wait_ge(weights_ready, 3)
            pe.transpose(MX[0][:, 0:n], ROWS[:, :], IDENT[0:n, 0:n]).then_inc(pe_const, 1)
            pe.wait_ge(cols_ready, 1)
            pe.wait_ge(weights_ready, 4)
            pe.wait_ge(ffn_loaded, 32)

            def ffn(r):
                pe.wait_ge(fv, 9 * r + 9)
                for n in range(TB):
                    last = pe.transpose(ACC[0][:, n * P:(n + 1) * P], LND[:, n, :], IDENT[:, :])
                last.then_inc(fp, 1)
                pe.wait_ge(xt_ready, r + 1)
                for n in range(TB):
                    last = pe.matmul(MX[0][:, n * E:(n + 1) * E], XT[:, n * P:(n + 1) * P],
                                     COLS[:, E * FC:E * FC + E], start=True, stop=True)
                last.then_inc(gate_logits, 1)

                def up(i):
                    w = 2 * E * r + i
                    c, e = divmod(i, E)
                    for f in range(FC):
                        if not (isinstance(r, int) and r == 0 and i == 0):
                            pe.wait_ge(silu_done, FC * (w - 1) + f + 1)
                        pe.matmul(up_bank(f), W1S[:, e, f * P:(f + 1) * P], XT[:, c * BANK:(c + 1) * BANK],
                                  start=True, stop=True).then_inc(up_done, 1)

                def down(i):
                    w = 2 * E * r + i
                    e = i % E
                    pe.wait_ge(silu_done, FC * w + FC)
                    if i < 2:
                        pe.wait_ge(gate_steps, 6 * r + 2)
                    if not (isinstance(r, int) and r == 0 and i < 2):
                        pe.wait_ge(y_added, w - 1)
                    for n in range(NT):
                        out_ = MX[i % 2][:, n * D:(n + 1) * D]
                        for f in range(FC):
                            pe.matmul(out_, HID[i % 2][:, f, n * P:(n + 1) * P], W2S[:, e, f, :],
                                      start=(f == 0), stop=False)
                        last = pe.matmul(out_, ONES[:, :], B2R[:, e, :], start=False, stop=True)
                    last.then_inc(down_done, 1)
                up(0)
                for i in range(1, 2 * E):
                    up(i)
                    down(i - 1)
                down(2 * E - 1)
            ffn(0)
            with pe.Fori(1, B) as r:
                ffn(r)
            for b in range(B):
                pe.wait_ge(ln_v, 6 * b + 6)
                if b > 0:
                    pe.wait_ge(yt_ready, b)
                for n in range(TB):
                    last = pe.transpose(ACC[0][:, n * P:(n + 1) * P], LND[:, n, :], IDENT[:, :])
                last.then_inc(ln_p, 1)
                pe.wait_ge(yt_ready, b + 1)
                if b > 0:
                    pe.wait_ge(val_copied, b)
                for half in range(NB):
                    last = pe.matmul(CT[:, half * BANK:(half + 1) * BANK], WVAL[:, :],
                                     YT[:, b * T + half * BANK:b * T + (half + 1) * BANK], start=True, stop=True)
                last.then_inc(val_done, 1)
            pe.wait_ge(val_copied, B)

            def project(u, b, hh, kind):
                if kind == 1:
                    pe.wait_ge(dve_args, DA * u + DA_DMG)
                elif not (isinstance(u, int) and u == 0):
                    pe.wait_ge(dve_args, DA * u)
                for half in range(NB):
                    last = pe.matmul(CT[:, half * BANK:(half + 1) * BANK], F[:, hh, kind, :],
                                     YT[:, bass.ds(b * T + half * BANK, BANK)], start=True, stop=True)
                last.then_inc(ct_ready, 1)

            def reduce(u, s):
                g, k = divmod(s, 4)
                first_unit = isinstance(u, int) and u == 0
                if k == 0:
                    if g < 2:
                        if not first_unit:
                            pe.wait_ge(bond_evac, 4 * u - 1 + g)
                    elif g < 6:
                        pe.wait_ge(tanh_done, 4 * u + g - 1)
                    else:
                        pe.wait_ge(bond_evac, 4 * u + g - 5)
                pe.wait_ge(gelu_done, 64 * u + 2 * s + 2)
                kind = 1 if g < GROUPS else 0
                for half in range(NB):
                    for q in range(4):
                        slot = A[(2 * s + q // 2) % RING]
                        last = pe.matmul(ACC[g % 2][32 * q:32 * q + 32, half * BANK:(half + 1) * BANK],
                                         WSEL[:, kind, k, :],
                                         slot[:, 1 - q % 2, half * BANK:(half + 1) * BANK],
                                         start=(k == 0), stop=(k == 3), tile_position=(0, 32 * q))
                last.then_inc(pe_used, 1)

            def tail(v, hh, s):
                lt = LT[hh]
                first = isinstance(v, int) and v == 0
                if s == 3:
                    pe.wait_ge(masked, v + 1)
                if 3 <= s <= 6:
                    for tb in (2 * (s - 3), 2 * (s - 3) + 1):
                        if tb == 1 and not first:
                            pe.wait_ge(x_added, 2 * v)
                        if tb >= 2:
                            pe.wait_ge(max_done, TB * v + tb - 1)
                        for jg in range(GROUPS):
                            last = pe.transpose(MX[tb % 2][:, jg * P:(jg + 1) * P],
                                                lt[:, jg, tb * P:(tb + 1) * P], IDENT[:, :])
                        last.then_inc(transposed, 1)
                if s == 8:
                    for half in range(2):
                        pe.wait_ge(mrep_done, 2 * v + half + 1)
                        for i in range(TB // 2):
                            last = pe.matmul(MX[half][:, i * P:(i + 1) * P],
                                             MREP[:, half * TB // 2 + i, :, :].rearrange("p j h -> p (j h)"),
                                             IDENT[:, :], start=True, stop=True)
                        last.then_inc(mbc_done, 1)
                if s in (11, 12):
                    half = s - 11
                    pe.wait_ge(exp_done, v + 1)
                    if half:
                        pe.wait_ge(recip_done, 2 * v + 1)
                    for jg in range(GROUPS):
                        last = pe.matmul(MX[1][:, :], SELALL[:, :], lt[:, jg, half * BANK:(half + 1) * BANK],
                                         start=(jg == 0), stop=(jg == GROUPS - 1))
                    last.then_inc(den_done, 1)
                i = s - 13 if 13 <= s <= 20 else s - 14 if 22 <= s <= 29 else None
                if i is not None:
                    half, e = divmod(i, HS)
                    pe.wait_ge(prod_done, 16 * v + i + 1)
                    if i == HS:
                        pe.wait_ge(norm_done, 2 * v + 1)
                    q = e // 2
                    for jg in range(GROUPS):
                        last = pe.matmul(MX[0][32 * q:32 * q + 32, :], SELE[:, e % 2, :], Y[i % 2][:, jg, :],
                                         start=(e % 2 == 0 and jg == 0), stop=(e % 2 == 1 and jg == GROUPS - 1),
                                         tile_position=(0, 32 * q))
                    last.then_inc(num_used, 1)
                if s in (24, 31):
                    half = (s - 24) // 7
                    pe.wait_ge(norm_done, 2 * v + half + 1)
                    pe.wait_ge(recip_done, 2 * v + 2)
                    if half:
                        pe.wait_ge(x_added, 2 * v + 1)
                    for i in range(TB // 2):
                        tok = (half * TB // 2 + i) * P
                        last = pe.matmul(MX[1][:, i * P:(i + 1) * P], O[:, tok:tok + P], WC[:, hh, :],
                                         start=True, stop=True)
                    last.then_inc(cproj_done, 1)

            def unit(u, b, hh, v, nxt):
                for s in range(STEPS):
                    if s == 14:
                        project(u, b, hh, 1)
                    if s == STEPS - 2 and nxt is not None:
                        project(u + 1, nxt, 1 - hh, 0)
                    if v is not None:
                        tail(v, 1 - hh, s)
                    reduce(u, s)
            project(0, 0, 0, 0)
            unit(0, 0, 0, None, 0)
            unit(1, 0, 1, 0, 1)
            with pe.Fori(1, B - 1) as b:
                unit(2 * b, b, 0, 2 * b - 1, b)
                unit(2 * b + 1, b, 1, 2 * b, b + 1)
            unit(2 * B - 2, B - 1, 0, 2 * B - 3, B - 1)
            unit(2 * B - 1, B - 1, 1, 2 * B - 2, None)
            for s in range(STEPS):
                tail(2 * B - 1, 1, s)
            pe.wait_ge(ffn_loaded, 64)
            with pe.Fori(B, 2 * B) as r:
                ffn(r)

_INS = ['L0_attn_x', 'L0_attn_W_disp', 'L0_attn_W_val', 'L0_attn_rel_pos_emb', 'L0_attn_W_strain', 'L0_attn_W_pos', 'L0_attn_W_bond', 'L0_attn_W_dmg', 'L0_attn_b_dmg', 'L0_attn_W_dmg_out', 'L0_attn_b_dmg_out', 'L0_attn_W_cproj', 'L0_ffn_rms_w', 'L0_ffn_gate_w', 'L0_ffn_W1', 'L0_ffn_b1', 'L0_ffn_W2', 'L0_ffn_b2']
_OUTS = [((4, 1024, 128), 'float32')]
def kernel(**inputs):
    import numpy as _np
    import concourse.bacc as _bacc
    from concourse import mybir as _mybir
    from concourse.bass_utils import run_bass_kernel_spmd as _run
    nc = _bacc.Bacc("TRN2", target_bir_lowering=False, num_devices=1)
    arrays, args = {}, []
    for name in _INS:
        a = _np.ascontiguousarray(inputs[name])
        arrays[f"in_{name}_dram"] = a
        args.append(nc.dram_tensor(f"in_{name}_dram", a.shape, _mybir.dt.from_np(a.dtype), kind="ExternalInput").ap())
    for i, (shape, dtype) in enumerate(_OUTS):
        dt = _mybir.dt.from_np(_np.dtype(dtype))
        args.append(nc.dram_tensor(f"out_{i}_dram", shape, dt, kind="ExternalOutput").ap())
    prog(nc, *args)
    r = _run(nc, [arrays], core_ids=[0])
    got = tuple(r.results[0][f"out_{i}_dram"] for i in range(len(_OUTS)))
    return got[0]
```

```python
import concourse.bass as bass
from concourse import mybir
from contextlib import ExitStack


def prog(nc, x, W_disp, W_val, rel_pos_emb, W_strain, W_pos, W_bond, W_dmg, b_dmg, W_dmg_out,
         b_dmg_out, W_cproj, rms_w, gate_w, W1, b1, W2, b2, out):
    fp32 = mybir.dt.float32
    i32 = mybir.dt.int32
    u32 = mybir.dt.uint32
    ALU = mybir.AluOpType
    ACT = mybir.ActivationFunctionType
    AX = mybir.AxisListType

    B, T, D = x.shape
    HORIZON, BD = rel_pos_emb.shape
    H = W_disp.shape[1] // BD
    HS = D // H
    P = 128
    TILES = B * T // P
    TB = T // P
    HH = P // BD
    HALVES = H // HH
    BANK = 512
    NB = T // BANK
    OFFS = 16
    GROUPS = HORIZON // OFFS
    PAD = HORIZON
    VPAD = OFFS * (GROUPS - 1)
    VW = VPAD + T
    VROW = PAD + T
    LN_EPS = 1e-5
    RMS_EPS = 1e-6
    E, _, FF = W1.shape
    FC = FF // P
    SORTED = TILES + E
    UNROLL = 8
    LOOPS = SORTED // UNROLL - 1

    PAIRS = OFFS // 2
    STEPS = 2 * GROUPS * PAIRS // 2
    RING = 8
    POOL_SLOTS = [8 * g + p for g, ps in enumerate(((2, 4, 7), (1, 3, 5, 7), (2, 4, 7), (1, 3, 5, 7)))
                  for p in ps]
    PA = len(POOL_SLOTS)
    DA_DMG = GROUPS * PAIRS - PA
    DA = DA_DMG + GROUPS * PAIRS

    ctx = ExitStack()
    with ctx:
        def sb(name, shape, dt=fp32):
            return ctx.enter_context(nc.sbuf_tensor(name, shape, dt))

        def pb(name, cols):
            return ctx.enter_context(nc.psum_tensor(name, [P, cols], fp32))

        def sem(name):
            return ctx.enter_context(nc.semaphore(name))

        def window(first, dims):
            return bass.AP(tensor=first.tensor, offset=first.offset, ap=[first.ap[0]] + dims)

        X = sb("X", [P, TILES, D])
        YT = sb("YT", [P, B * T])
        A = [sb(f"A{i}", [P, 2, T]) for i in range(RING)]
        DPAD = sb("DPAD", [P, PAD + T])
        SPAD = sb("SPAD", [P, PAD + T])
        LT = [sb(f"LT{i}", [P, GROUPS, T]) for i in range(HALVES)]
        WFF = sb("WFF", [P, HS * VW])
        VSH = WFF[:, :].rearrange("p (e w) -> p e w", e=HS)
        W1S = WFF[:, 0:E * FF].rearrange("p (e f) -> p e f", e=E)
        W2AT = E * FF
        W2S = WFF[:, W2AT:W2AT + E * FF].rearrange("p (e c d) -> p e c d", e=E, c=FC)
        Y = [sb(f"Y{i}", [P, GROUPS, BANK]) for i in range(2)]
        RD = sb("RD", [P, T])
        O = sb("O", [P, T])
        M8 = sb("M8", [P, TB, HH])
        MREP = O[:, :].rearrange("p (n j h) -> p n j h", j=OFFS, h=HH)
        YF = [y[:, :, :].rearrange("p g t -> p (g t)") for y in Y]
        VS = YF[1][:, 0:T]
        STAT = sb("STAT", [P, 5, TILES])
        NEGHALF = sb("NEGHALF", [P, TILES])
        U = LT[0][:, :, :].rearrange("p g t -> p (g t)").rearrange("p (n d) -> p n d", d=D)
        SQ = LT[1][:, :, :].rearrange("p g t -> p (g t)").rearrange("p (n d) -> p n d", d=D)
        B1S = YT
        B2S = O
        AF = [a[:, :, :].rearrange("p i t -> p (i t)") for a in A]
        UT = [AF[2][:, 0:T], AF[3][:, 0:T]]
        GT = [AF[5][:, i * TILES * E:(i + 1) * TILES * E].rearrange("p (n e) -> p n e", e=E)
              for i in range(8)]
        XS = [AF[4][:, i * D:(i + 1) * D] for i in range(UNROLL)]
        XST = [AF[6][:, i * P:(i + 1) * P] for i in range(2)]
        HB = [AF[7][:, i * FF:(i + 1) * FF] for i in range(2)]
        HS_ = [AF[0][:, i * FF:(i + 1) * FF] for i in range(2)]
        HST = [AF[1][:, i * FF:(i + 1) * FF] for i in range(2)]
        YB = [AF[6][:, (2 + i) * D:(3 + i) * D] for i in range(4)]
        POS = sb("POS", [P, TILES], u32)
        SCORE = sb("SCORE", [P, TILES])
        SMALL = sb("SMALL", [P, 6, E])
        CNTI = sb("CNTI", [P, E], i32)
        EIDF = sb("EIDF", [P, SORTED])
        EID = sb("EID", [P, SORTED], i32)
        ONES = sb("ONES", [P, P])
        TRI = sb("TRI", [P, P])
        ROWS = sb("ROWS", [E + 1, D])
        COLS = sb("COLS", [P, E + 1])
        GATEW = sb("GATEW", [P, E])
        IT = sb("IT", [P, 4], i32)
        ITF = sb("ITF", [P, 4])
        scratch = A[0][:, 0, :].bitcast(i32)
        COLI = scratch[:, 0:128]
        COLHI = scratch[:, 128:256]
        COLBI = scratch[:, 256:384]
        CMI = scratch[:, 384:384 + GROUPS * PAD].rearrange("p (g t) -> p g t", g=GROUPS)
        COLH = A[1][:, 0, 0:128]
        COLB = A[1][:, 0, 128:256]
        COL = sb("COL", [P, 128])
        CMASK = sb("CMASK", [P, GROUPS, PAD])
        IDENT = sb("IDENT", [P, P])
        SELALL = sb("SELALL", [P, P])
        SELE = sb("SELE", [P, 2, 32])
        WSEL = sb("WSEL", [P, 2, 4, 32])
        WCOL = sb("WCOL", [P, 2])
        BDMG = sb("BDMG", [P, 1])
        BOUT = sb("BOUT", [P, 1])
        BOUTH = sb("BOUTH", [P, 1])
        WREP = sb("WREP", [P, 2, BD])
        BDW = A[7][:, 1, 4 * P:6 * P].rearrange("p (k c) -> p k c", k=2)
        REL = sb("REL", [HORIZON, BD])
        RELT = sb("RELT", [BD, HORIZON])
        WPOS = sb("WPOS", [BD, BD])
        WPOSR = sb("WPOSR", [BD, HH, BD])
        PCOL = sb("PCOL", [P, HORIZON])
        WDISP = A[7][:, 1, 0:HALVES * P]
        WDT = A[7][:, 1, HALVES * P:2 * HALVES * P].rearrange("p (h c) -> p h c", h=HALVES)
        F = sb("F", [P, HALVES, 2, P])
        WVAL = sb("WVAL", [P, D])
        WC = sb("WC", [P, HALVES, D])
        ZP = sb("ZP", [P, PAD])

        CT = pb("CT", T)
        ACC = [pb("ACC0", T), pb("ACC1", T)]
        MX = [pb("MX0", BANK), pb("MX1", BANK)]

        xs_d = nc.dram_tensor("sorted_tokens", (SORTED * P, D), fp32, kind="Internal").ap()
        ys_d = nc.dram_tensor("sorted_outputs", (SORTED * P, D), fp32, kind="Internal").ap()
        vd = nc.dram_tensor("values_scratch", (B, D, VROW), fp32, kind="Internal").ap()

        x_loaded = sem("x_loaded")
        w_loaded = sem("w_loaded")
        pool_const = sem("pool_const")
        dve_const = sem("dve_const")
        pe_const = sem("pe_const")
        consts_ready = sem("consts_ready")
        weights_ready = sem("weights_ready")
        yt_ready = sem("yt_ready")
        norm_sums = sem("norm_sums")
        norm_means = sem("norm_means")
        norm_centred = sem("norm_centred")
        norm_squares = sem("norm_squares")
        norm_vars = sem("norm_vars")
        norm_small = sem("norm_small")
        norm_pow = sem("norm_pow")
        norm_ready = sem("norm_ready")
        u_transposed = sem("u_transposed")
        u_evacuated = sem("u_evacuated")
        gate_logits = sem("gate_logits")
        gate_exp = sem("gate_exp")
        route_steps = sem("route_steps")
        onehot_ready = sem("onehot_ready")
        gate_shifted = sem("gate_shifted")
        ranks_done = sem("ranks_done")
        route_ready = sem("route_ready")
        ffn_loaded = sem("ffn_loaded")
        xs_cleared = sem("xs_cleared")
        scattered = sem("scattered")
        gathered = [sem(f"gathered{i}") for i in range(B)]
        x_arrived = [sem(f"x_arrived{i}") for i in range(UNROLL)]
        y_stored = [sem(f"y_stored{i}") for i in range(4)]
        x_turned = sem("x_turned")
        xt_ready = sem("xt_ready")
        up_done = sem("up_done")
        biased = sem("biased")
        silu_done = sem("silu_done")
        h_turned = sem("h_turned")
        ht_ready = sem("ht_ready")
        down_done = sem("down_done")
        y_ready = sem("y_ready")
        ffn_added = sem("ffn_added")
        rms_steps = sem("rms_steps")
        eid_ready = sem("eid_ready")
        val_done = sem("val_done")
        val_copied = sem("val_copied")
        val_stored = sem("val_stored")
        ct_ready = sem("ct_ready")
        pad_ready = sem("pad_ready")
        dve_args = sem("dve_args")
        pool_args = sem("pool_args")
        gelu_done = sem("gelu_done")
        pe_used = sem("pe_used")
        tanh_done = sem("tanh_done")
        bond_evac = sem("bond_evac")
        masked = sem("masked")
        transposed = sem("transposed")
        max_done = sem("max_done")
        mrep_done = sem("mrep_done")
        mbc_done = sem("mbc_done")
        shifted = sem("shifted")
        exp_done = sem("exp_done")
        den_done = sem("den_done")
        recip_done = sem("recip_done")
        vsh_loaded = sem("vsh_loaded")
        prod_done = sem("prod_done")
        num_used = sem("num_used")
        norm_done = sem("norm_done")
        cproj_done = sem("cproj_done")
        x_added = sem("x_added")
        out_stored = sem("out_stored")

        def later(sem_name, engine, ph, i, c, back):
            if ph > 0 or not isinstance(i, int) or UNROLL * i + c - back >= 0:
                engine.wait_ge(sem_name, ph * SORTED + UNROLL * i + c - back + 1)

        def slots(engine, slot):
            for c in range(-2, UNROLL + 1):
                slot(0, c)
            with engine.Fori(1, LOOPS) as i:
                for c in range(1, UNROLL + 1):
                    slot(i, c)
            for c in range(1, UNROLL + 1):
                slot(LOOPS, c)

        def inside(i, c):
            return not isinstance(i, int) or 0 <= UNROLL * i + c < SORTED

        def experts_of(engine, i, c):
            return [engine.value_load(EID[0:1, bass.ds(UNROLL * i + c + d, 1)], min_val=0, max_val=E - 1)
                    if inside(i, c + d) else None for d in (1, -1)]

        block = ctx.enter_context(nc.Block())

        WL = 16 * (2 + 1 + 8 + 8 + 8 + 8 + 8 + 1 + 1 + 1 + 1 + 16 + 1)

        @block.sync
        def _(sp):
            for b in range(B):
                sp.dma_start(X[:, b * TB:(b + 1) * TB, :],
                             x[b].rearrange("(n p) d -> p n d", p=P)).then_inc(x_loaded, 16)
            sp.dma_start(ROWS[0:E, :], gate_w).then_inc(w_loaded, 16)
            sp.dma_start(ROWS[E:E + 1, :], rms_w.unsqueeze(0)).then_inc(w_loaded, 16)
            sp.dma_start(WDISP[:, :], W_disp).then_inc(w_loaded, 16)
            for h in range(HH):
                rows = slice(h * BD, (h + 1) * BD)
                sp.dma_start(WREP[rows, 0, :], W_strain).then_inc(w_loaded, 16)
                sp.dma_start(WREP[rows, 1, :], W_dmg).then_inc(w_loaded, 16)
                sp.dma_start(WCOL[rows, 0:1], W_bond).then_inc(w_loaded, 16)
                sp.dma_start(WCOL[rows, 1:2], W_dmg_out).then_inc(w_loaded, 16)
                sp.dma_start(BDMG[rows, :], b_dmg.unsqueeze(1)).then_inc(w_loaded, 16)
            sp.dma_start(REL[:, :], rel_pos_emb).then_inc(w_loaded, 16)
            sp.dma_start(WPOS[:, :], W_pos).then_inc(w_loaded, 16)
            sp.dma_start(WVAL[:, :], W_val).then_inc(w_loaded, 16)
            sp.dma_start(BOUT[:, :], b_dmg_out.partition_broadcast(P)).then_inc(w_loaded, 16)
            sp.wait_ge(dve_const, 1)
            for hh in range(HALVES):
                for e in range(HS):
                    row = 32 * (e // 2) + 8 * (e % 2)
                    sp.dma_start(WC[row:row + HH, hh, :],
                                 W_cproj.rearrange("(h e) d -> e h d", e=HS)[e, hh * HH:(hh + 1) * HH, :]
                                 ).then_inc(w_loaded, 16)
            sp.wait_ge(dve_const, 2)
            sp.dma_start(vd[:, :, 0:PAD].rearrange("b c w -> c b w"),
                         ZP[:, :].unsqueeze(1).broadcast_to([P, B, PAD])).then_inc(w_loaded, 16)

            sp.wait_ge(dve_const, 3)
            sp.dma_start(xs_d.rearrange("(n p) d -> p n d", p=P),
                         TRI[:, :].unsqueeze(1).broadcast_to([P, SORTED, D])).then_inc(xs_cleared, 16)

            def load_experts():
                sp.dma_start(W1S, W1.rearrange("e d f -> d e f")).then_inc(ffn_loaded, 16)
                for e in range(E):
                    sp.dma_start(W2S[:, e, :, :], W2[e].rearrange("(c f) d -> f c d", c=FC)
                                 ).then_inc(ffn_loaded, 16)
                sp.dma_start(B1S[:, :], b1.rearrange("e f -> (e f)").partition_broadcast(P)
                             ).then_inc(ffn_loaded, 16)
                sp.dma_start(B2S[:, :], b2.rearrange("e d -> (e d)").partition_broadcast(P)
                             ).then_inc(ffn_loaded, 16)

            def sorted_tiles(ph):
                def load(i, c):
                    later(x_turned, sp, ph, i, c, UNROLL)
                    sp.dma_start(XS[c % UNROLL], xs_d[bass.ds((UNROLL * i + c) * P, P), :]
                                 ).then_inc(x_arrived[c % UNROLL], 16)

                def store(i, c):
                    later(y_ready, sp, ph, i, c, 0)
                    sp.dma_start(ys_d[bass.ds((UNROLL * i + c) * P, P), :], YB[c % 4]
                                 ).then_inc(y_stored[c % 4], 16)
                sp.wait_ge(scattered, 16 * TILES * (ph + 1))
                for c in range(UNROLL):
                    load(0, c)
                with sp.Fori(0, LOOPS) as i:
                    for c in range(UNROLL):
                        store(i, c)
                        load(i, c + UNROLL)
                for c in range(UNROLL):
                    store(LOOPS, c)
            load_experts()
            sorted_tiles(0)

            def store_values(b):
                sp.wait_ge(val_copied, b + 1)
                sp.dma_start(vd[b, :, PAD:VROW], VS[:, :]).then_inc(val_stored, 16)
            for b in range(B):
                store_values(b)
            sp.wait_ge(val_stored, 16 * B)
            sp.wait_ge(w_loaded, WL)

            def load_values(b, hh, u):
                if not (isinstance(u, int) and u == 0):
                    sp.wait_ge(prod_done, 16 * u)
                else:
                    sp.wait_ge(down_done, SORTED)
                for j in range(OFFS):
                    row = 32 * (j % 4) + 8 * (j // 4)
                    first = PAD - VPAD - j
                    src = vd[b, hh * HH * HS:(hh + 1) * HH * HS, first:first + VW]
                    sp.dma_start(VSH[row:row + HH, :, :], src.rearrange("(h e) w -> h e w", e=HS)
                                 ).then_inc(vsh_loaded, 16)

            def store(b):
                sp.wait_ge(ffn_added, TILES + (b + 1) * TB)
                sp.dma_start(out[b].rearrange("(n p) d -> p n d", p=P),
                             X[:, b * TB:(b + 1) * TB, :]).then_inc(out_stored, 16)
            for hh in range(HALVES):
                load_values(0, hh, hh)
            with sp.Fori(1, B) as b:
                for hh in range(HALVES):
                    load_values(b, hh, 2 * b + hh)
            sp.wait_ge(prod_done, 16 * 2 * B)
            sp.wait_ge(x_added, 4 * B)
            load_experts()
            sorted_tiles(1)
            for b in range(B):
                store(b)
            sp.wait_ge(out_stored, 16 * B)

        @block.gpsimd
        def _(pool):
            pool.iota(IT[:, 0:1], [[0, 1]], base=0, channel_multiplier=1).then_inc(pool_const, 1)
            pool.iota(COLI[:, :], [[1, 128]], base=0, channel_multiplier=0).then_inc(pool_const, 1)
            pool.iota(COLHI[:, :], [[0, 16], [1, 8]], base=0, channel_multiplier=0).then_inc(pool_const, 1)
            pool.iota(COLBI[:, :], [[1, 8], [0, 16]], base=0, channel_multiplier=0).then_inc(pool_const, 1)
            pool.iota(CMI[:, :, :], [[-OFFS, GROUPS], [1, PAD]], base=0, channel_multiplier=0
                      ).then_inc(pool_const, 1)
            pool.memset(NEGHALF[:, :], -0.5).then_inc(pool_const, 1)
            pool.wait_ge(pool_const, 6)
            def power(small):
                pool.wait_ge(norm_small, small)
                pool.tensor_tensor(STAT[:, 3, :], STAT[:, 2, :], NEGHALF[:, :], ALU.pow).then_inc(norm_pow, 1)

            def scatter(ph):
                pool.wait_ge(route_ready, ph + 1)
                pool.wait_ge(xs_cleared, 16)
                for n in range(TILES):
                    pool.indirect_dma_start(
                        out=xs_d, out_offset=bass.IndirectOffsetOnAxis(POS[:, n:n + 1], 0),
                        in_=U[:, n, :], in_offset=None).then_inc(scattered, 16)

            def gather(ph):
                for r in range(4):
                    pool.wait_ge(y_stored[r], 16 * (SORTED // 4) * (ph + 1))
                for n in range(TILES):
                    pool.indirect_dma_start(
                        out=SQ[:, n, :], out_offset=None, in_=ys_d,
                        in_offset=bass.IndirectOffsetOnAxis(POS[:, n:n + 1], 0)).then_inc(gathered[n // TB], 16)
            power(1)
            power(3)
            scatter(0)
            gather(0)
            power(4)

            def difference(u, g, p):
                n = 8 * g + p
                pool.wait_ge(pad_ready, 2 * u + 1)
                if not (isinstance(u, int) and u == 0 and n < RING):
                    pool.wait_ge(pe_used, 32 * u + (n - RING) // 2 + 1)
                j = OFFS * g + 2 * p
                pool.tensor_tensor(A[n % RING][:, :, :], window(DPAD[:, PAD - j - 1:PAD - j], [[1, 2], [1, T]]),
                                   window(DPAD[:, PAD:PAD + 1], [[0, 2], [1, T]]), ALU.subtract).then_inc(pool_args, 1)

            def product(v, hh, i):
                half, e = divmod(i, HS)
                first = VPAD + half * BANK
                if i == 0:
                    pool.wait_ge(exp_done, v + 1)
                    pool.wait_ge(vsh_loaded, 16 * OFFS * (v + 1))
                if not (isinstance(v, int) and v == 0 and i < 2):
                    pool.wait_ge(num_used, 16 * v + i - 1)
                pool.tensor_tensor(Y[i % 2][:, :, :], LT[hh][:, :, half * BANK:(half + 1) * BANK],
                                   window(VSH[:, e, first:first + 1], [[-OFFS, GROUPS], [1, BANK]]),
                                   ALU.mult).then_inc(prod_done, 1)

            def unit(u, hh, v):
                for n in POOL_SLOTS:
                    difference(u, *divmod(n, PAIRS))
                if v is not None:
                    for i in range(2 * HS):
                        product(v, 1 - hh, i)
            unit(0, 0, None)
            unit(1, 1, 0)
            with pool.Fori(1, B) as b:
                for hh in range(HALVES):
                    unit(2 * b + hh, hh, 2 * b + hh - 1)
            for i in range(2 * HS):
                product(2 * B - 1, 1, i)
            power(5)
            power(7)
            scatter(1)
            gather(1)

        @block.scalar
        def _(act):
            def squares(r):
                for b in range(B):
                    act.wait_ge(norm_centred, B * r + b + 1)
                    act.activation(SQ[:, b * TB:(b + 1) * TB, :], U[:, b * TB:(b + 1) * TB, :], ACT.Square
                                   ).then_inc(norm_squares, 1)

            def ffn(ph):
                squares(2 * ph)
                for b in range(B):
                    act.wait_ge(u_transposed, 2 * B * ph + b + 1)
                    if b >= 2:
                        act.wait_ge(gate_logits, B * ph + b - 1)
                    act.activation(UT[b % 2], ACC[b % 2][:, :], ACT.Copy).then_inc(u_evacuated, 1)
                act.wait_ge(gate_shifted, ph + 1)
                act.activation(GT[1], GT[0], ACT.Exp).then_inc(gate_exp, 1)

                def slot(i, c):
                    if inside(i, c + 1):
                        later(biased, act, ph, i, c + 1, 0)
                        later(h_turned, act, ph, i, c + 1, 2)
                        act.activation(HS_[(c + 1) % 2], HB[(c + 1) % 2], ACT.Silu).then_inc(silu_done, 1)
                    if inside(i, c):
                        later(h_turned, act, ph, i, c, 0)
                        later(down_done, act, ph, i, c, 2)
                        act.activation(HST[c % 2], ACC[0][:, (c % 2) * BANK:(c % 2 + 1) * BANK], ACT.Copy
                                       ).then_inc(ht_ready, 1)
                slots(act, slot)
            ffn(0)
            act.wait_ge(dve_const, 3)
            squares(1)
            for b in range(B):
                act.wait_ge(val_done, b + 1)
                if b > 0:
                    act.wait_ge(val_stored, 16 * b)
                act.activation(VS[:, :], CT[:, :], ACT.Copy).then_inc(val_copied, 1)

            def gelu(u, g, p):
                n = 8 * g + p
                by_pool = sum(1 for s in POOL_SLOTS if s < n)
                if n in POOL_SLOTS:
                    act.wait_ge(pool_args, PA * u + by_pool + 1)
                else:
                    act.wait_ge(dve_args, DA * u + n - by_pool + 1)
                bias = BDMG[:, :] if g < GROUPS else 0.0
                act.activation(A[n % RING][:, :, :], A[n % RING][:, :, :], ACT.Gelu, bias=bias
                               ).then_inc(gelu_done, 1)

            def damage(u, hh, g):
                act.wait_ge(pe_used, 4 * (8 * u + g + 1))
                act.activation(LT[hh][:, g, :], ACC[g % 2][:, :], ACT.Tanh, bias=BOUTH[:, :], scale=0.5
                               ).then_inc(tanh_done, 1)

            def exponentials(v, hh):
                act.wait_ge(shifted, 2 * v + 2)
                act.activation(LT[hh][:, :, :], LT[hh][:, :, :], ACT.Exp).then_inc(exp_done, 1)

            def unit(u, hh, v):
                for g in range(2 * GROUPS):
                    for p in range(PAIRS):
                        if v is not None and 8 * g + p == 24:
                            exponentials(v, 1 - hh)
                        if 1 <= g <= GROUPS and p == 4:
                            damage(u, hh, g - 1)
                        gelu(u, g, p)
            unit(0, 0, None)
            unit(1, 1, 0)
            with act.Fori(1, B) as b:
                for hh in range(HALVES):
                    unit(2 * b + hh, hh, 2 * b + hh - 1)
            exponentials(2 * B - 1, 1)
            ffn(1)

        @block.vector
        def _(dve):
            dve.memset(WC[:, :, :], 0.0).then_inc(dve_const, 1)
            dve.memset(ZP[:, :], 0.0).then_inc(dve_const, 1)
            dve.memset(TRI[:, :], 0.0).then_inc(dve_const, 1)
            dve.wait_ge(w_loaded, WL)
            dve.tensor_scalar(BOUTH[:, :], BOUT[:, :], 0.5, None, ALU.mult).then_inc(dve_const, 1)
            done = [4]

            def step(ins):
                ins.then_inc(dve_const, 1)
                done[0] += 1
                dve.wait_ge(dve_const, done[0])
            step(dve.memset(DPAD[:, 0:PAD], 0.0))
            step(dve.memset(SPAD[:, 0:PAD], 0.0))
            step(dve.memset(ONES[:, :], 1.0))
            dve.wait_ge(pool_const, 6)
            step(dve.tensor_scalar(IT[:, 1:2], IT[:, 0:1], 5, None, ALU.logical_shift_right))
            step(dve.tensor_scalar(IT[:, 2:3], IT[:, 0:1], 3, 3, ALU.logical_shift_right, ALU.bitwise_and))
            step(dve.tensor_scalar(ITF[:, 0:1], IT[:, 2:3], 4.0, None, ALU.mult))
            step(dve.tensor_copy(ITF[:, 1:2], IT[:, 1:2]))
            step(dve.tensor_tensor(ITF[:, 0:1], ITF[:, 0:1], ITF[:, 1:2], ALU.add))
            step(dve.tensor_scalar(IT[:, 3:4], IT[:, 0:1], 7, None, ALU.bitwise_and))
            step(dve.tensor_copy(ITF[:, 1:2], IT[:, 3:4]))
            step(dve.tensor_scalar(IT[:, 3:4], IT[:, 0:1], 4, None, ALU.logical_shift_right))
            step(dve.tensor_copy(ITF[:, 2:3], IT[:, 3:4]))
            step(dve.tensor_copy(ITF[:, 3:4], IT[:, 0:1]))
            step(dve.tensor_copy(COL[:, :], COLI[:, :]))
            step(dve.tensor_copy(COLH[:, :], COLHI[:, :]))
            step(dve.tensor_copy(COLB[:, :], COLBI[:, :]))
            step(dve.tensor_copy(CMASK[:, :, :], CMI[:, :, :]))
            step(dve.tensor_scalar(CMASK[:, :, :], CMASK[:, :, :], ITF[:, 0:1], -1e30, ALU.is_lt, ALU.mult))
            step(dve.tensor_scalar(IDENT[:, :], COL[:, :], ITF[:, 3:4], None, ALU.is_equal))
            step(dve.tensor_scalar(SELALL[:, :], COLH[:, :], ITF[:, 1:2], None, ALU.is_equal))
            dve.wait_ge(xs_cleared, 16)
            step(dve.tensor_scalar(TRI[:, :], COL[:, :], ITF[:, 3:4], None, ALU.is_gt))
            for par in range(2):
                step(dve.tensor_scalar(SELE[:, par, :], COL[:, 0:32], -8.0 * par, ITF[:, 1:2], ALU.add,
                                       ALU.is_equal))
            for kind in range(2):
                for k in range(4):
                    step(dve.tensor_scalar(WSEL[:, kind, k, :], COL[:, 0:32], -8.0 * k, ITF[:, 2:3],
                                           ALU.add, ALU.is_equal))
                    step(dve.tensor_scalar(WSEL[:, kind, k, :], WSEL[:, kind, k, :], WCOL[:, kind:kind + 1],
                                           None, ALU.mult))
            step(dve.tensor_scalar(COLB[:, :], COLB[:, :], ITF[:, 2:3], None, ALU.is_equal))
            for kind in range(2):
                step(dve.tensor_tensor(BDW[:, kind, :].rearrange("p (h c) -> p h c", c=BD),
                                       COLB[:, :].rearrange("p (h c) -> p h c", c=BD),
                                       WREP[:, kind, :].unsqueeze(1).broadcast_to([P, HH, BD]), ALU.mult))
            dve.tensor_copy(WPOSR[:, :, :], WPOS[:, :].unsqueeze(1).broadcast_to([BD, HH, BD])
                            ).then_inc(consts_ready, 1)
            dve.wait_ge(pe_const, 1)
            dve.tensor_copy(RELT[:, :], MX[0][0:BD, 0:HORIZON]).then_inc(weights_ready, 1)
            dve.wait_ge(pe_const, 2)
            dve.tensor_copy(WDT[:, :, :].rearrange("p h c -> p (h c)"), MX[1][:, 0:HALVES * P]).then_inc(weights_ready, 1)
            dve.wait_ge(pe_const, 3)
            dve.tensor_copy(PCOL[:, :], MX[0][:, 0:HORIZON]).then_inc(weights_ready, 1)
            dve.wait_ge(pe_const, 4)
            dve.tensor_copy(F[:, :, :, :].rearrange("p h k c -> p (h k c)"), MX[1][:, :]).then_inc(weights_ready, 1)

            dve.wait_ge(pe_const, 5)
            dve.tensor_copy(COLS[:, :], MX[0][:, 0:E + 1]).then_inc(weights_ready, 1)
            dve.wait_ge(weights_ready, 5)
            dve.tensor_scalar(GATEW[:, :], COLS[:, 0:E], COLS[:, E:E + 1], None, ALU.mult
                              ).then_inc(weights_ready, 1)

            def wide(row, b):
                return STAT[:, row, b * TB:(b + 1) * TB].unsqueeze(2).broadcast_to([P, TB, D])

            def norm(r, small, pows, rms):
                batch = [slice(b * TB, (b + 1) * TB) for b in range(B)]
                for b in range(B):
                    dve.tensor_reduce(STAT[:, 0, batch[b]], X[:, batch[b], :], AX.X, ALU.add
                                      ).then_inc(norm_sums, 1)
                dve.wait_ge(norm_sums, B * (r + 1))
                dve.tensor_scalar(STAT[:, 1, :], STAT[:, 0, :], 1.0 / D, None, ALU.mult).then_inc(norm_means, 1)
                dve.wait_ge(norm_means, r + 1)
                for b in range(B):
                    dve.tensor_tensor(U[:, batch[b], :], X[:, batch[b], :], wide(1, b), ALU.subtract
                                      ).then_inc(norm_centred, 1)
                for b in range(B):
                    dve.wait_ge(norm_squares, B * r + b + 1)
                    dve.tensor_reduce(STAT[:, 4, batch[b]], SQ[:, batch[b], :], AX.X, ALU.add
                                      ).then_inc(norm_vars, 1)
                dve.wait_ge(norm_vars, B * (r + 1))
                dve.tensor_scalar(STAT[:, 2, :], STAT[:, 4, :], 1.0 / D, LN_EPS, ALU.mult, ALU.add
                                  ).then_inc(norm_small, 1)
                dve.wait_ge(norm_pow, pows + 1)
                scale = 3
                if rms:
                    dve.tensor_tensor(STAT[:, 1, :], STAT[:, 3, :], STAT[:, 3, :], ALU.mult
                                      ).then_inc(rms_steps, 1)
                    dve.wait_ge(rms_steps, r // 2 * 3 + 1)
                    dve.tensor_tensor(STAT[:, 1, :], STAT[:, 1, :], STAT[:, 4, :], ALU.mult
                                      ).then_inc(rms_steps, 1)
                    dve.tensor_copy(STAT[:, 0, :], STAT[:, 3, :]).then_inc(norm_small, 1)
                    dve.wait_ge(norm_small, small + 2)
                    dve.wait_ge(rms_steps, r // 2 * 3 + 2)
                    dve.tensor_scalar(STAT[:, 2, :], STAT[:, 1, :], 1.0 / D, RMS_EPS, ALU.mult, ALU.add
                                      ).then_inc(norm_small, 1)
                    dve.wait_ge(norm_pow, pows + 2)
                    dve.tensor_tensor(STAT[:, 0, :], STAT[:, 0, :], STAT[:, 3, :], ALU.mult
                                      ).then_inc(rms_steps, 1)
                    dve.wait_ge(rms_steps, r // 2 * 3 + 3)
                    scale = 0
                for b in range(B):
                    dve.tensor_tensor(U[:, batch[b], :], U[:, batch[b], :], wide(scale, b), ALU.mult
                                      ).then_inc(norm_ready, 1)

            routed = [0]

            def rstep(ins):
                ins.then_inc(route_steps, 1)
                routed[0] += 1
                dve.wait_ge(route_steps, routed[0])

            def spread(table):
                return table.unsqueeze(2).broadcast_to([P, TILES, E])

            def route(ph):
                dve.wait_ge(gate_logits, B * (ph + 1))
                lg = MX[0][:, 0:TILES * E].rearrange("p (n e) -> p n e", e=E)
                rstep(dve.tensor_reduce(STAT[:, 0, :], lg, AX.X, ALU.max))
                dve.tensor_tensor(GT[0], lg, spread(STAT[:, 0, :]), ALU.subtract).then_inc(gate_shifted, 1)
                dve.wait_ge(gate_shifted, ph + 1)
                rstep(dve.tensor_scalar(GT[2], GT[0], 0.0, -16.0, ALU.is_ge, ALU.mult))
                rstep(dve.tensor_tensor(GT[2], GT[2], COL[:, 0:E].unsqueeze(1).broadcast_to([P, TILES, E]),
                                        ALU.add))
                rstep(dve.tensor_reduce(STAT[:, 1, :], GT[2], AX.X, ALU.min))
                dve.tensor_tensor(GT[3], GT[2], spread(STAT[:, 1, :]), ALU.is_equal).then_inc(onehot_ready, 1)
                dve.wait_ge(onehot_ready, ph + 1)
                dve.wait_ge(gate_exp, ph + 1)
                rstep(dve.tensor_reduce(STAT[:, 2, :], GT[1], AX.X, ALU.add))
                rstep(dve.reciprocal(STAT[:, 3, :], STAT[:, 2, :]))
                rstep(dve.tensor_scalar(SCORE[:, :], STAT[:, 3, :], 0.5, None, ALU.mult))
                dve.wait_ge(ranks_done, ph + 1)
                before = MX[1][:, 0:TILES * E].rearrange("p (n e) -> p n e", e=E)
                rstep(dve.tensor_copy(GT[4], MX[1][:, TILES * E:2 * TILES * E].rearrange(
                    "p (n e) -> p n e", e=E)))
                src, dst, reach = 4, 5, 1
                while reach < TILES:
                    dve.tensor_copy(GT[dst][:, 0:reach, :], GT[src][:, 0:reach, :])
                    rstep(dve.tensor_tensor(GT[dst][:, reach:TILES, :], GT[src][:, reach:TILES, :],
                                            GT[src][:, 0:TILES - reach, :], ALU.add))
                    src, dst, reach = dst, (6 if dst == 5 else 5), 2 * reach
                total = GT[src][:, TILES - 1, :]
                rstep(dve.tensor_scalar(CNTI[:, :], total, float(P - 1), None, ALU.add))
                rstep(dve.tensor_scalar(CNTI[:, :], CNTI[:, :], P.bit_length() - 1, None,
                                        ALU.logical_shift_right))
                rstep(dve.tensor_copy(SMALL[:, 0, :], CNTI[:, :]))
                last, reach = 0, 1
                while reach < E:
                    dve.tensor_copy(SMALL[:, last + 1, 0:reach], SMALL[:, last, 0:reach])
                    rstep(dve.tensor_tensor(SMALL[:, last + 1, reach:E], SMALL[:, last, reach:E],
                                            SMALL[:, last, 0:E - reach], ALU.add))
                    last, reach = last + 1, 2 * reach
                ends = SMALL[:, last, :]
                rstep(dve.tensor_tensor(SMALL[:, 4, :], ends, SMALL[:, 0, :], ALU.subtract))
                rstep(dve.tensor_scalar(SMALL[:, 5, :], SMALL[:, 4, :], float(P), None, ALU.mult))
                rstep(dve.tensor_tensor(GT[7], GT[src], GT[4], ALU.subtract))
                rstep(dve.tensor_tensor(GT[7], GT[7], before, ALU.add))
                rstep(dve.tensor_tensor(GT[7], GT[7], SMALL[:, 5, :].unsqueeze(1).broadcast_to([P, TILES, E]),
                                        ALU.add))
                rstep(dve.tensor_tensor(GT[7], GT[7], GT[3], ALU.mult))
                rstep(dve.tensor_reduce(STAT[:, 0, :], GT[7], AX.X, ALU.add))
                dve.tensor_copy(POS[:, :], STAT[:, 0, :]).then_inc(route_ready, 1)
                marks = AF[2][:, 0:SORTED * E].rearrange("p (k e) -> p k e", e=E)
                rstep(dve.tensor_tensor(marks, COL[:, 0:SORTED].unsqueeze(2).broadcast_to([P, SORTED, E]),
                                        ends.unsqueeze(1).broadcast_to([P, SORTED, E]), ALU.is_ge))
                rstep(dve.tensor_reduce(EIDF[:, :], marks, AX.X, ALU.add))
                dve.tensor_scalar(EID[:, :], EIDF[:, :], float(E - 1), None, ALU.min).then_inc(eid_ready, 1)
                dve.wait_ge(eid_ready, ph + 1)

            def experts(ph):
                dve.wait_ge(ffn_loaded, 16 * (E + 3) * (ph + 1))

                def slot(i, c):
                    e_up, e_down = experts_of(dve, i, c)
                    if inside(i, c + 2):
                        k = (c + 2) % 2
                        later(x_turned, dve, ph, i, c + 2, 0)
                        later(up_done, dve, ph, i, c + 2, 2)
                        dve.tensor_scalar(XST[k], MX[k][:, 0:P], COLS[:, E:E + 1], None, ALU.mult
                                          ).then_inc(xt_ready, 1)
                    if inside(i, c + 1):
                        k = (c + 1) % 2
                        later(up_done, dve, ph, i, c + 1, 0)
                        later(silu_done, dve, ph, i, c + 1, 2)
                        dve.tensor_tensor(HB[k], CT[:, k * BANK:(k + 1) * BANK], B1S[:, bass.ds(e_up * FF, FF)],
                                          ALU.add).then_inc(biased, 1)
                    if inside(i, c - 1):
                        k = (c - 1) % 4
                        later(down_done, dve, ph, i, c - 1, 0)
                        if ph > 0 or not isinstance(i, int) or UNROLL * i + c - 5 >= 0:
                            dve.wait_ge(y_stored[k], 16 * ((SORTED // 4) * ph + 2 * i + (c - 1) // 4))
                        at = ((c - 1) % 2) * BANK
                        dve.tensor_tensor(YB[k], ACC[1][:, at:at + D], B2S[:, bass.ds(e_down * D, D)],
                                          ALU.add).then_inc(y_ready, 1)
                slots(dve, slot)
                for n in range(TILES):
                    if n % TB == 0:
                        dve.wait_ge(gathered[n // TB], 16 * TB * (ph + 1))
                    dve.scalar_tensor_tensor(X[:, n, :], SQ[:, n, :], SCORE[:, n:n + 1], X[:, n, :],
                                             ALU.mult, ALU.add).then_inc(ffn_added, 1)
            dve.wait_ge(x_loaded, 16 * B)
            norm(0, 0, 0, True)
            route(0)
            experts(0)
            dve.wait_ge(ffn_added, TILES)
            norm(1, 3, 2, False)
            for b in range(B):
                dve.wait_ge(u_transposed, B + b + 1)
                dve.tensor_copy(YT[:, b * T:(b + 1) * T], ACC[b % 2][:, :]).then_inc(yt_ready, 1)

            def copy_pad(u, kind):
                dve.wait_ge(ct_ready, 2 * u + kind + 1)
                if kind == 0 and not (isinstance(u, int) and u == 0):
                    dve.wait_ge(pool_args, PA * u)
                dve.tensor_copy((DPAD, SPAD)[kind][:, PAD:PAD + T], CT[:, :]).then_inc(pad_ready, 1)
                dve.wait_ge(pad_ready, 2 * u + kind + 1)

            def difference(u, g, p):
                n = 8 * g + p
                if not (isinstance(u, int) and u == 0 and n < RING):
                    dve.wait_ge(pe_used, 32 * u + (n - RING) // 2 + 1)
                slot = A[n % RING]
                j = OFFS * (g % GROUPS) + 2 * p
                if g < GROUPS:
                    dve.tensor_tensor(slot[:, :, :], window(DPAD[:, PAD - j - 1:PAD - j], [[1, 2], [1, T]]),
                                      window(CT[:, 0:1], [[0, 2], [1, T]]), ALU.subtract).then_inc(dve_args, 1)
                else:
                    for i in range(2):
                        ji = j + 1 - i
                        last = dve.scalar_tensor_tensor(
                            slot[:, i, :], SPAD[:, PAD - ji:PAD - ji + T],
                            PCOL[:, HORIZON - 1 - ji:HORIZON - ji], CT[:, :], ALU.add, ALU.subtract)
                    last.then_inc(dve_args, 1)

            def logits(u, hh, g):
                dve.wait_ge(pe_used, 4 * (8 * u + g + 1))
                dve.wait_ge(tanh_done, 4 * u + g - 3)
                lt = LT[hh][:, g - GROUPS, :]
                dve.scalar_tensor_tensor(lt, lt, -5.0, ACC[g % 2][:, :], ALU.mult, ALU.add
                                         ).then_inc(bond_evac, 1)

            def tail(v, vb, hh, s):
                lt = LT[hh]
                if s == 3:
                    logits(v, hh, 2 * GROUPS - 1)
                    dve.wait_ge(bond_evac, 4 * v + 4)
                    dve.tensor_tensor(lt[:, :, 0:PAD], lt[:, :, 0:PAD], CMASK[:, :, :], ALU.add
                                      ).then_inc(masked, 1)
                if 7 <= s <= 10:
                    for tb in (2 * (s - 7), 2 * (s - 7) + 1):
                        dve.wait_ge(transposed, TB * v + tb + 1)
                        dve.tensor_reduce(M8[:, tb, :], MX[tb % 2][:, :].rearrange("p (j h) -> p h j", h=HH),
                                          AX.X, ALU.max).then_inc(max_done, 1)
                if s == 10:
                    dve.wait_ge(max_done, TB * (v + 1))
                    for i in range(2):
                        blocks = slice(i * TB // 2, (i + 1) * TB // 2)
                        last = dve.tensor_copy(MREP[:, blocks, :, :],
                                               M8[:, blocks, :].unsqueeze(2).broadcast_to([P, TB // 2, OFFS, HH]))
                        last.then_inc(mrep_done, 1)
                if s == 12:
                    for half in range(2):
                        dve.wait_ge(mbc_done, 2 * v + half + 1)
                        cols = slice(half * BANK, (half + 1) * BANK)
                        dve.tensor_tensor(lt[:, :, cols], lt[:, :, cols],
                                          window(MX[half][:, 0:1], [[0, GROUPS], [1, BANK]]), ALU.subtract
                                          ).then_inc(shifted, 1)
                if s in (18, 21):
                    half = (s - 18) // 3
                    dve.wait_ge(den_done, 2 * v + half + 1)
                    dve.reciprocal(RD[:, half * BANK:(half + 1) * BANK], MX[1][:, :]).then_inc(recip_done, 1)
                if s in (25, 33):
                    half = (s - 25) // 8
                    cols = slice(half * BANK, (half + 1) * BANK)
                    dve.wait_ge(num_used, 16 * v + 8 * (half + 1))
                    if half == 0:
                        dve.wait_ge(recip_done, 2 * v + 2)
                        if not (isinstance(v, int) and v == 0):
                            dve.wait_ge(cproj_done, 2 * v)
                    dve.tensor_tensor(O[:, cols], MX[0][:, :], RD[:, cols], ALU.mult).then_inc(norm_done, 1)
                if s in (31, 36):
                    half = (s - 31) // 5
                    dve.wait_ge(cproj_done, 2 * v + half + 1)
                    first = vb * TB + half * TB // 2
                    xs = X[:, bass.ds(first, TB // 2), :]
                    dve.tensor_tensor(xs, xs, MX[1][:, :].rearrange("p (n d) -> p n d", d=D), ALU.add
                                      ).then_inc(x_added, 1)

            def unit(u, hh, v, vb, v2, vb2):
                copy_pad(u, 0)
                for g in range(2 * GROUPS):
                    if g == GROUPS:
                        copy_pad(u, 1)
                    for p in range(PAIRS):
                        if PAIRS * g + p not in POOL_SLOTS:
                            difference(u, g, p)
                        if GROUPS + 1 <= g and p == (7 if g == 2 * GROUPS - 1 else 4):
                            logits(u, hh, g - 1)
                        if p % 2 == 1:
                            s = 4 * g + p // 2
                            if s < 5 and v2 is not None:
                                tail(v2, vb2, hh, STEPS + s)
                            if v is not None:
                                tail(v, vb, 1 - hh, s)
            unit(0, 0, None, None, None, None)
            unit(1, 1, 0, 0, None, None)
            with dve.Fori(1, B) as b:
                unit(2 * b, 0, 2 * b - 1, b - 1, 2 * b - 2, b - 1)
                unit(2 * b + 1, 1, 2 * b, b, 2 * b - 1, b - 1)
            for s in range(STEPS, STEPS + 5):
                tail(2 * B - 2, B - 1, 0, s)
            for s in range(STEPS + 5):
                tail(2 * B - 1, B - 1, 1, s)
            dve.wait_ge(x_added, 4 * B)
            norm(2, 4, 3, True)
            route(1)
            experts(1)

        @block.tensor
        def _(pe):
            pe.wait_ge(consts_ready, 1)
            pe.wait_ge(w_loaded, WL)
            pe.transpose(MX[0][0:BD, 0:HORIZON], REL[:, :], IDENT[0:HORIZON, 0:HORIZON]).then_inc(pe_const, 1)
            for hh in range(HALVES):
                last = pe.transpose(MX[1][:, hh * P:(hh + 1) * P], WDISP[:, hh * P:(hh + 1) * P], IDENT[:, :])
            last.then_inc(pe_const, 1)
            pe.wait_ge(weights_ready, 2)
            pe.matmul(MX[0][:, 0:HORIZON], WPOSR[:, :, :].rearrange("p h c -> p (h c)"), RELT[:, :],
                      start=True, stop=True).then_inc(pe_const, 1)
            for hh in range(HALVES):
                for kind in range(2):
                    col = (2 * hh + kind) * P
                    last = pe.matmul(MX[1][:, col:col + P], WDT[:, hh, :], BDW[:, 1 - kind, :],
                                     start=True, stop=True)
            last.then_inc(pe_const, 1)
            pe.wait_ge(weights_ready, 3)
            pe.transpose(MX[0][:, 0:E + 1], ROWS[:, :], IDENT[0:E + 1, 0:E + 1]).then_inc(pe_const, 1)
            pe.wait_ge(weights_ready, 6)

            def turn(r, b):
                pe.wait_ge(norm_ready, B * r + b + 1)
                for n in range(TB):
                    last = pe.transpose(ACC[b % 2][:, n * P:(n + 1) * P], U[:, b * TB + n, :], IDENT[:, :])
                last.then_inc(u_transposed, 1)

            def ffn(ph):
                for b in range(B):
                    if b >= 2:
                        pe.wait_ge(u_evacuated, B * ph + b - 1)
                    turn(2 * ph, b)
                for b in range(B):
                    pe.wait_ge(u_evacuated, B * ph + b + 1)
                    for n in range(TB):
                        at = (b * TB + n) * E
                        last = pe.matmul(MX[0][:, at:at + E], UT[b % 2][:, n * P:(n + 1) * P], GATEW[:, :],
                                         start=True, stop=True)
                    last.then_inc(gate_logits, 1)
                pe.wait_ge(onehot_ready, ph + 1)
                onehot = GT[3].rearrange("p n e -> p (n e)")
                pe.matmul(MX[1][:, 0:TILES * E], TRI[:, :], onehot, start=True, stop=True)
                pe.matmul(MX[1][:, TILES * E:2 * TILES * E], ONES[:, :], onehot, start=True, stop=True
                          ).then_inc(ranks_done, 1)
                pe.wait_ge(eid_ready, ph + 1)
                pe.wait_ge(ffn_loaded, 16 * (E + 3) * (ph + 1))

                def slot(i, c):
                    e_up, e_down = experts_of(pe, i, c)
                    if inside(i, c + 2):
                        k = (c + 2) % 2
                        pe.wait_ge(x_arrived[(c + 2) % UNROLL],
                                   16 * ((SORTED // UNROLL) * ph + i + (c + 2) // UNROLL + 1))
                        later(xt_ready, pe, ph, i, c + 2, 2)
                        pe.transpose(MX[k][:, 0:P], XS[(c + 2) % UNROLL], IDENT[:, :]).then_inc(x_turned, 1)
                    if inside(i, c + 1):
                        k = (c + 1) % 2
                        later(xt_ready, pe, ph, i, c + 1, 0)
                        later(biased, pe, ph, i, c + 1, 2)
                        pe.matmul(CT[:, k * BANK:(k + 1) * BANK], XST[k], WFF[:, bass.ds(e_up * FF, FF)],
                                  start=True, stop=True).then_inc(up_done, 1)
                    if inside(i, c):
                        k = c % 2
                        later(silu_done, pe, ph, i, c, 0)
                        later(ht_ready, pe, ph, i, c, 2)
                        for f in range(FC):
                            at = k * BANK + f * P
                            last = pe.transpose(ACC[0][:, at:at + P], HS_[k][:, f * P:(f + 1) * P], IDENT[:, :])
                        last.then_inc(h_turned, 1)
                    if inside(i, c - 1):
                        k = (c - 1) % 2
                        later(ht_ready, pe, ph, i, c - 1, 0)
                        later(y_ready, pe, ph, i, c - 1, 2)
                        for f in range(FC):
                            last = pe.matmul(ACC[1][:, k * BANK:k * BANK + D], HST[k][:, f * P:(f + 1) * P],
                                             WFF[:, bass.ds(W2AT + e_down * FF + f * D, D)],
                                             start=(f == 0), stop=(f == FC - 1))
                        last.then_inc(down_done, 1)
                slots(pe, slot)
            ffn(0)
            for b in range(B):
                if b >= 2:
                    pe.wait_ge(yt_ready, b - 1)
                turn(1, b)
            for b in range(B):
                pe.wait_ge(yt_ready, b + 1)
                if b > 0:
                    pe.wait_ge(val_copied, b)
                for half in range(NB):
                    last = pe.matmul(CT[:, half * BANK:(half + 1) * BANK], WVAL[:, :],
                                     YT[:, b * T + half * BANK:b * T + (half + 1) * BANK], start=True, stop=True)
                last.then_inc(val_done, 1)
            pe.wait_ge(val_copied, B)

            def project(u, b, hh, kind):
                if kind == 1:
                    pe.wait_ge(dve_args, DA * u + DA_DMG)
                elif not (isinstance(u, int) and u == 0):
                    pe.wait_ge(dve_args, DA * u)
                for half in range(NB):
                    last = pe.matmul(CT[:, half * BANK:(half + 1) * BANK], F[:, hh, kind, :],
                                     YT[:, bass.ds(b * T + half * BANK, BANK)], start=True, stop=True)
                last.then_inc(ct_ready, 1)

            def reduce(u, s):
                g, k = divmod(s, 4)
                first_unit = isinstance(u, int) and u == 0
                if k == 0:
                    if g < 2:
                        if not first_unit:
                            pe.wait_ge(bond_evac, 4 * u - 1 + g)
                    elif g < 6:
                        pe.wait_ge(tanh_done, 4 * u + g - 1)
                    else:
                        pe.wait_ge(bond_evac, 4 * u + g - 5)
                pe.wait_ge(gelu_done, 64 * u + 2 * s + 2)
                kind = 1 if g < GROUPS else 0
                for half in range(NB):
                    for q in range(4):
                        slot = A[(2 * s + q // 2) % RING]
                        last = pe.matmul(ACC[g % 2][32 * q:32 * q + 32, half * BANK:(half + 1) * BANK],
                                         WSEL[:, kind, k, :],
                                         slot[:, 1 - q % 2, half * BANK:(half + 1) * BANK],
                                         start=(k == 0), stop=(k == 3), tile_position=(0, 32 * q))
                last.then_inc(pe_used, 1)

            def tail(v, hh, s):
                lt = LT[hh]
                first = isinstance(v, int) and v == 0
                if s == 5:
                    pe.wait_ge(masked, v + 1)
                if 5 <= s <= 8:
                    for tb in (2 * (s - 5), 2 * (s - 5) + 1):
                        if tb == 1 and not first:
                            pe.wait_ge(x_added, 2 * v)
                        if tb >= 2:
                            pe.wait_ge(max_done, TB * v + tb - 1)
                        for jg in range(GROUPS):
                            last = pe.transpose(MX[tb % 2][:, jg * P:(jg + 1) * P],
                                                lt[:, jg, tb * P:(tb + 1) * P], IDENT[:, :])
                        last.then_inc(transposed, 1)
                if s == 10:
                    for half in range(2):
                        pe.wait_ge(mrep_done, 2 * v + half + 1)
                        for i in range(TB // 2):
                            last = pe.matmul(MX[half][:, i * P:(i + 1) * P],
                                             MREP[:, half * TB // 2 + i, :, :].rearrange("p j h -> p (j h)"),
                                             IDENT[:, :], start=True, stop=True)
                        last.then_inc(mbc_done, 1)
                if s in (14, 17):
                    half = (s - 14) // 3
                    pe.wait_ge(exp_done, v + 1)
                    if half:
                        pe.wait_ge(recip_done, 2 * v + 1)
                    for jg in range(GROUPS):
                        last = pe.matmul(MX[1][:, :], SELALL[:, :], lt[:, jg, half * BANK:(half + 1) * BANK],
                                         start=(jg == 0), stop=(jg == GROUPS - 1))
                    last.then_inc(den_done, 1)
                i = s - 15 if 15 <= s <= 22 else s - 16 if 24 <= s <= 31 else None
                if i is not None:
                    half, e = divmod(i, HS)
                    pe.wait_ge(prod_done, 16 * v + i + 1)
                    if i == HS:
                        pe.wait_ge(norm_done, 2 * v + 1)
                    q = e // 2
                    for jg in range(GROUPS):
                        last = pe.matmul(MX[0][32 * q:32 * q + 32, :], SELE[:, e % 2, :], Y[i % 2][:, jg, :],
                                         start=(e % 2 == 0 and jg == 0), stop=(e % 2 == 1 and jg == GROUPS - 1),
                                         tile_position=(0, 32 * q))
                    last.then_inc(num_used, 1)
                if s in (27, 34):
                    half = (s - 27) // 7
                    pe.wait_ge(norm_done, 2 * v + half + 1)
                    pe.wait_ge(recip_done, 2 * v + 2)
                    if half:
                        pe.wait_ge(x_added, 2 * v + 1)
                    for i in range(TB // 2):
                        tok = (half * TB // 2 + i) * P
                        last = pe.matmul(MX[1][:, i * P:(i + 1) * P], O[:, tok:tok + P], WC[:, hh, :],
                                         start=True, stop=True)
                    last.then_inc(cproj_done, 1)

            def unit(u, b, hh, v, v2, nxt):
                for s in range(STEPS):
                    if s == 12:
                        project(u, b, hh, 1)
                    if s == STEPS - 2 and nxt is not None:
                        project(u + 1, nxt, 1 - hh, 0)
                    if v2 is not None and s < 3:
                        tail(v2, hh, STEPS + s)
                    if v is not None:
                        tail(v, 1 - hh, s)
                    reduce(u, s)
            project(0, 0, 0, 0)
            unit(0, 0, 0, None, None, 0)
            unit(1, 0, 1, 0, None, 1)
            with pe.Fori(1, B - 1) as b:
                unit(2 * b, b, 0, 2 * b - 1, 2 * b - 2, b)
                unit(2 * b + 1, b, 1, 2 * b, 2 * b - 1, b + 1)
            unit(2 * B - 2, B - 1, 0, 2 * B - 3, 2 * B - 4, B - 1)
            unit(2 * B - 1, B - 1, 1, 2 * B - 2, 2 * B - 3, None)
            for s in range(STEPS, STEPS + 3):
                tail(2 * B - 2, 0, s)
            for s in range(STEPS + 3):
                tail(2 * B - 1, 1, s)
            ffn(1)

_INS = ['L0_attn_x', 'L0_attn_W_disp', 'L0_attn_W_val', 'L0_attn_rel_pos_emb', 'L0_attn_W_strain', 'L0_attn_W_pos', 'L0_attn_W_bond', 'L0_attn_W_dmg', 'L0_attn_b_dmg', 'L0_attn_W_dmg_out', 'L0_attn_b_dmg_out', 'L0_attn_W_cproj', 'L0_ffn_rms_w', 'L0_ffn_gate_w', 'L0_ffn_W1', 'L0_ffn_b1', 'L0_ffn_W2', 'L0_ffn_b2']
_OUTS = [((4, 1024, 128), 'float32')]
def kernel(**inputs):
    import numpy as _np
    import concourse.bacc as _bacc
    from concourse import mybir as _mybir
    from concourse.bass_utils import run_bass_kernel_spmd as _run
    nc = _bacc.Bacc("TRN2", target_bir_lowering=False, num_devices=1)
    arrays, args = {}, []
    for name in _INS:
        a = _np.ascontiguousarray(inputs[name])
        arrays[f"in_{name}_dram"] = a
        args.append(nc.dram_tensor(f"in_{name}_dram", a.shape, _mybir.dt.from_np(a.dtype), kind="ExternalInput").ap())
    for i, (shape, dtype) in enumerate(_OUTS):
        dt = _mybir.dt.from_np(_np.dtype(dtype))
        args.append(nc.dram_tensor(f"out_{i}_dram", shape, dt, kind="ExternalOutput").ap())
    prog(nc, *args)
    r = _run(nc, [arrays], core_ids=[0])
    got = tuple(r.results[0][f"out_{i}_dram"] for i in range(len(_OUTS)))
    return got[0]
```

```python
import concourse.bass as bass
from concourse import mybir
from contextlib import ExitStack


def prog(nc, x, W_disp, W_val, rel_pos_emb, W_strain, W_pos, W_bond, W_dmg, b_dmg, W_dmg_out,
         b_dmg_out, W_cproj, rms_w, gate_w, W1, b1, W2, b2, out):
    fp32 = mybir.dt.float32
    i32 = mybir.dt.int32
    u32 = mybir.dt.uint32
    ALU = mybir.AluOpType
    ACT = mybir.ActivationFunctionType
    AX = mybir.AxisListType

    B, T, D = x.shape
    HORIZON, BD = rel_pos_emb.shape
    H = W_disp.shape[1] // BD
    HS = D // H
    P = 128
    TILES = B * T // P
    TB = T // P
    HH = P // BD
    HALVES = H // HH
    BANK = 512
    NB = T // BANK
    OFFS = 16
    GROUPS = HORIZON // OFFS
    PAD = HORIZON
    VPAD = OFFS * (GROUPS - 1)
    VW = VPAD + T
    VROW = PAD + T
    LN_EPS = 1e-5
    RMS_EPS = 1e-6
    E, _, FF = W1.shape
    FC = FF // P
    SORTED = TILES + E
    UNROLL = 8
    LOOPS = SORTED // UNROLL - 1

    PAIRS = OFFS // 2
    STEPS = 2 * GROUPS * PAIRS // 2
    RING = 8
    POOL_SLOTS, PRODUCTS_AHEAD = zip(*(
        (2, 0), (4, 0), (6, 0), (7, 0), (16, 0), (18, 0), (20, 0), (22, 0), (23, 0), (33, 1), (36, 2)))
    PA = len(POOL_SLOTS)
    DA = 2 * GROUPS * PAIRS - PA

    SHIFT_AT, EXP_AT, SPREAD_AT, RD_AT = 12, 24, 43, (46, 50)

    ctx = ExitStack()
    with ctx:
        def sb(name, shape, dt=fp32):
            return ctx.enter_context(nc.sbuf_tensor(name, shape, dt))

        def pb(name, cols):
            return ctx.enter_context(nc.psum_tensor(name, [P, cols], fp32))

        def sem(name):
            return ctx.enter_context(nc.semaphore(name))

        def window(first, dims):
            return bass.AP(tensor=first.tensor, offset=first.offset, ap=[first.ap[0]] + dims)

        X = sb("X", [P, TILES, D])
        YT = sb("YT", [P, B * T])
        A = [sb(f"A{i}", [P, 2, T]) for i in range(RING)]
        DPAD = sb("DPAD", [P, PAD + T])
        SPAD = sb("SPAD", [P, PAD + T])
        LTF = [sb("LT0", [P, TILES * (D + 1)]), sb("LT1", [P, GROUPS * T])]
        LT = [lt[:, 0:GROUPS * T].rearrange("p (g t) -> p g t", g=GROUPS)
              for lt in LTF]
        WFF = sb("WFF", [P, HS * VW])
        VSH = WFF[:, :].rearrange("p (e w) -> p e w", e=HS)
        W1S = WFF[:, 0:E * FF].rearrange("p (e f) -> p e f", e=E)
        W2AT = E * FF
        W2S = WFF[:, W2AT:W2AT + E * FF].rearrange("p (e c d) -> p e c d", e=E, c=FC)
        Y = [sb(f"Y{i}", [P, GROUPS, BANK]) for i in range(2)]
        RD = sb("RD", [P, T])
        O = sb("O", [P, T])
        M8 = sb("M8", [P, TB, HH])
        R8 = sb("R8", [P, TB, HH])
        SPREAD = O[:, :].rearrange("p (n j h) -> p n j h", j=OFFS, h=HH)
        YF = [y[:, :, :].rearrange("p g t -> p (g t)") for y in Y]
        VS = YF[1][:, 0:T]
        SPARE = YF[0][:, 0:UNROLL * (D + 1)]
        SPAREN = SPARE.rearrange("p (n d) -> p n d", d=D + 1)
        STAT = sb("STAT", [P, 6, TILES])
        UID = LTF[0][:, :].rearrange("p (n d) -> p n d", d=D + 1)
        U = UID[:, :, 0:D]
        YG = LTF[1][:, :].rearrange("p (n d) -> p n d", d=D)
        B1S = YT
        B2S = O
        AF = [a[:, :, :].rearrange("p i t -> p (i t)") for a in A]
        NSQ = [AF[6][:, 0:T].rearrange("p (n d) -> p n d", d=D),
               AF[7][:, 0:T].rearrange("p (n d) -> p n d", d=D)]
        UT = [AF[2][:, 0:T], AF[3][:, 0:T]]
        GT = [AF[5][:, i * TILES * E:(i + 1) * TILES * E].rearrange("p (n e) -> p n e", e=E)
              for i in range(8)]
        XS = [AF[4][:, i * (D + 1):(i + 1) * (D + 1)] for i in range(UNROLL)]
        XST = [AF[6][:, i * P:(i + 1) * P] for i in range(2)]
        HB = [AF[7][:, i * FF:(i + 1) * FF] for i in range(2)]
        HS_ = [AF[0][:, i * FF:(i + 1) * FF] for i in range(2)]
        HST = [AF[1][:, i * FF:(i + 1) * FF] for i in range(2)]
        YB = [AF[6][:, (2 + i) * D:(3 + i) * D] for i in range(4)]
        POS = sb("POS", [P, TILES], u32)
        SCORE = sb("SCORE", [P, TILES])
        SMALL = sb("SMALL", [P, 6, E])
        CNTI = sb("CNTI", [P, E], i32)
        EIDF = sb("EIDF", [P, SORTED])
        EID = sb("EID", [P, SORTED], i32)
        ONES = sb("ONES", [P, P])
        TRI = sb("TRI", [P, P])
        ROWS = sb("ROWS", [E + 1, D])
        COLS = sb("COLS", [P, E + 1])
        GATEW = sb("GATEW", [P, E])
        IT = sb("IT", [P, 4], i32)
        ITF = sb("ITF", [P, 4])
        scratch = A[0][:, 0, :].bitcast(i32)
        COLI = scratch[:, 0:128]
        COLHI = scratch[:, 128:256]
        COLBI = scratch[:, 256:384]
        CMI = scratch[:, 384:384 + GROUPS * PAD].rearrange("p (g t) -> p g t", g=GROUPS)
        COLH = A[1][:, 0, 0:128]
        COLB = A[1][:, 0, 128:256]
        COL = sb("COL", [P, 128])
        CMASK = sb("CMASK", [P, GROUPS, PAD])
        IDENT = sb("IDENT", [P, P])
        SELALL = sb("SELALL", [P, P])
        SELE = sb("SELE", [P, 2, 32])
        MINUS5 = sb("MINUS5", [P, P])
        WSEL = sb("WSEL", [P, 2, 4, 32])
        WCOL = sb("WCOL", [P, 2])
        BDMG = sb("BDMG", [P, 1])
        BOUT = sb("BOUT", [P, 1])
        BOUTH = sb("BOUTH", [P, 1])
        WREP = sb("WREP", [P, 2, BD])
        BDW = A[7][:, 1, 4 * P:6 * P].rearrange("p (k c) -> p k c", k=2)
        REL = sb("REL", [HORIZON, BD])
        RELT = sb("RELT", [BD, HORIZON])
        WPOS = sb("WPOS", [BD, BD])
        WPOSR = sb("WPOSR", [BD, HH, BD])
        PCOL = sb("PCOL", [P, HORIZON])
        WDISP = A[7][:, 1, 0:HALVES * P]
        WDT = A[7][:, 1, HALVES * P:2 * HALVES * P].rearrange("p (h c) -> p h c", h=HALVES)
        F = sb("F", [P, HALVES, 2, P])
        WVAL = sb("WVAL", [P, D])
        WC = sb("WC", [P, HALVES, D])
        ZP = sb("ZP", [P, PAD])

        CT = pb("CT", T)
        ACC = [pb("ACC0", T), pb("ACC1", T)]
        PROJ = [CT, ACC[1]]
        SUMS = ACC[0]
        MX = [pb("MX0", BANK), pb("MX1", BANK)]

        xs_d = nc.dram_tensor("sorted_tokens", (SORTED * P, D + 1), fp32, kind="Internal").ap()
        ys_d = nc.dram_tensor("expert_outputs", (B * T + UNROLL * P, D), fp32, kind="Internal").ap()
        vd = nc.dram_tensor("values_scratch", (B, D, VROW), fp32, kind="Internal").ap()

        x_loaded = [sem(f"x_loaded{b}") for b in range(B)]
        w_loaded = sem("w_loaded")
        pool_const = sem("pool_const")
        dve_const = sem("dve_const")
        pe_const = sem("pe_const")
        consts_ready = sem("consts_ready")
        weights_ready = sem("weights_ready")
        yt_ready = sem("yt_ready")
        norm_sums = sem("norm_sums")
        norm_means = sem("norm_means")
        norm_centred = sem("norm_centred")
        norm_squares = sem("norm_squares")
        norm_vars = sem("norm_vars")
        norm_args = sem("norm_args")
        norm_roots = sem("norm_roots")
        norm_newton = sem("norm_newton")
        norm_ready = sem("norm_ready")
        u_transposed = sem("u_transposed")
        u_evacuated = sem("u_evacuated")
        gate_logits = sem("gate_logits")
        gate_exp = sem("gate_exp")
        route_steps = sem("route_steps")
        onehot_ready = sem("onehot_ready")
        gate_shifted = sem("gate_shifted")
        ranks_done = sem("ranks_done")
        route_ready = sem("route_ready")
        ffn_loaded = sem("ffn_loaded")
        xs_cleared = sem("xs_cleared")
        scattered = sem("scattered")
        numbered = sem("numbered")
        spare_cleared = sem("spare_cleared")
        spare_ready = sem("spare_ready")
        y_loaded = [sem(f"y_loaded{i}") for i in range(B)]
        x_arrived = [sem(f"x_arrived{i}") for i in range(UNROLL)]
        y_stored = [sem(f"y_stored{i}") for i in range(4)]
        x_turned = sem("x_turned")
        xt_ready = sem("xt_ready")
        up_done = sem("up_done")
        biased = sem("biased")
        silu_done = sem("silu_done")
        h_turned = sem("h_turned")
        ht_ready = sem("ht_ready")
        down_done = sem("down_done")
        y_ready = sem("y_ready")
        ffn_added = sem("ffn_added")
        dve_products = sem("dve_products")
        consts_ffn = sem("consts_ffn")
        rows_loaded = sem("rows_loaded")
        eid_ready = sem("eid_ready")
        val_done = sem("val_done")
        val_copied = sem("val_copied")
        val_stored = sem("val_stored")
        ct_ready = sem("ct_ready")
        pad_ready = sem("pad_ready")
        dve_args = sem("dve_args")
        pool_args = sem("pool_args")
        gelu_done = sem("gelu_done")
        pe_used = sem("pe_used")
        tanh_done = sem("tanh_done")
        bond_evac = sem("bond_evac")
        masked = sem("masked")
        transposed = sem("transposed")
        max_done = sem("max_done")
        max_spread = sem("max_spread")
        recip_spread = sem("recip_spread")
        mbc_done = sem("mbc_done")
        shifted = sem("shifted")
        exp_done = sem("exp_done")
        den_done = sem("den_done")
        recip_done = sem("recip_done")
        rbc_done = sem("rbc_done")
        rd_ready = sem("rd_ready")
        vsh_loaded = sem("vsh_loaded")
        prod_done = sem("prod_done")
        num_used = sem("num_used")
        norm_done = sem("norm_done")
        cproj_done = sem("cproj_done")
        x_added = sem("x_added")
        out_stored = sem("out_stored")

        def later(sem_name, engine, ph, i, c, back):
            if ph > 0 or not isinstance(i, int) or UNROLL * i + c - back >= 0:
                engine.wait_ge(sem_name, ph * SORTED + UNROLL * i + c - back + 1)

        def slots(engine, slot):
            for i in (0, None, LOOPS):
                held = {}
                if i is None:
                    with engine.Fori(1, LOOPS) as i:
                        for c in range(1, UNROLL + 1):
                            slot(i, c, held)
                else:
                    for c in range(1 if i else -2, UNROLL + 1):
                        slot(i, c, held)

        def inside(i, c):
            return not isinstance(i, int) or 0 <= UNROLL * i + c < SORTED

        def experts_of(engine, i, c, held):
            for t in (c + 1, c - 1):
                if inside(i, t) and t not in held:
                    held[t] = engine.value_load(EID[0:1, bass.ds(UNROLL * i + t, 1)], min_val=0, max_val=E - 1)
            return held.get(c + 1), held.get(c - 1)

        block = ctx.enter_context(nc.Block())

        WL = 16 * (1 + 8 + 8 + 8 + 8 + 8 + 1 + 1 + 1 + 1 + 16 + 1)

        @block.sync
        def _(sp):
            for b in range(B):
                sp.dma_start(X[:, b * TB:(b + 1) * TB, :],
                             x[b].rearrange("(n p) d -> p n d", p=P)).then_inc(x_loaded[b], 16)
                if b == 0:
                    sp.dma_start(ROWS[0:E, :], gate_w).then_inc(rows_loaded, 16)
                    sp.dma_start(ROWS[E:E + 1, :], rms_w.unsqueeze(0)).then_inc(rows_loaded, 16)
            sp.wait_ge(spare_ready, 1)

            def clear_sorted():
                sp.dma_start(xs_d.rearrange("(g p n) d -> p g (n d)", p=P, n=UNROLL),
                             SPARE.unsqueeze(1).broadcast_to([P, SORTED // UNROLL, UNROLL * (D + 1)])
                             ).then_inc(xs_cleared, 16)

            def load_experts():
                sp.dma_start(W1S, W1.rearrange("e d f -> d e f")).then_inc(ffn_loaded, 16)
                for e in range(E):
                    sp.dma_start(W2S[:, e, :, :], W2[e].rearrange("(c f) d -> f c d", c=FC)
                                 ).then_inc(ffn_loaded, 16)
                sp.dma_start(B1S[:, :], b1.rearrange("e f -> (e f)").partition_broadcast(P)
                             ).then_inc(ffn_loaded, 16)
                sp.dma_start(B2S[:, :], b2.rearrange("e d -> (e d)").partition_broadcast(P)
                             ).then_inc(ffn_loaded, 16)

            clear_sorted()
            load_experts()
            sp.dma_start(WDISP, W_disp).then_inc(w_loaded, 16)
            for h in range(HH):
                rows = slice(h * BD, (h + 1) * BD)
                sp.dma_start(WREP[rows, 0, :], W_strain).then_inc(w_loaded, 16)
                sp.dma_start(WREP[rows, 1, :], W_dmg).then_inc(w_loaded, 16)
                sp.dma_start(WCOL[rows, 0:1], W_bond).then_inc(w_loaded, 16)
                sp.dma_start(WCOL[rows, 1:2], W_dmg_out).then_inc(w_loaded, 16)
                sp.dma_start(BDMG[rows, :], b_dmg.unsqueeze(1)).then_inc(w_loaded, 16)
            sp.dma_start(REL[:, :], rel_pos_emb).then_inc(w_loaded, 16)
            sp.dma_start(WPOS[:, :], W_pos).then_inc(w_loaded, 16)
            sp.dma_start(WVAL[:, :], W_val).then_inc(w_loaded, 16)
            sp.dma_start(BOUT[:, :], b_dmg_out.partition_broadcast(P)).then_inc(w_loaded, 16)
            sp.wait_ge(dve_const, 3)
            for hh in range(HALVES):
                for e in range(HS):
                    row = 32 * (e // 2) + 8 * (e % 2)
                    sp.dma_start(WC[row:row + HH, hh, :],
                                 W_cproj.rearrange("(h e) d -> e h d", e=HS)[e, hh * HH:(hh + 1) * HH, :]
                                 ).then_inc(w_loaded, 16)
            sp.dma_start(vd[:, :, 0:PAD].rearrange("b c w -> c b w"),
                         ZP[:, :].unsqueeze(1).broadcast_to([P, B, PAD])).then_inc(w_loaded, 16)

            def sorted_tiles(ph):
                sp.wait_ge(scattered, 16 * TILES * (ph + 1))
                for c in range(UNROLL):
                    sp.dma_start(XS[c], xs_d[c * P:(c + 1) * P, :]).then_inc(x_arrived[c], 16)
                with sp.Fori(0, LOOPS) as i:
                    for c in range(UNROLL):
                        sp.wait_ge(y_stored[c % 4], 16 * ((SORTED // 4) * ph + 2 * i + c // 4 + 1))
                        sp.dma_start(XS[c], xs_d[bass.ds((UNROLL * i + UNROLL + c) * P, P), :]
                                     ).then_inc(x_arrived[c], 16)
                for k in range(4):
                    sp.wait_ge(y_stored[k], 16 * (SORTED // 4) * (ph + 1))
                for b in range(B):
                    sp.dma_start(YG[:, b * TB:(b + 1) * TB, :],
                                 ys_d[b * T:(b + 1) * T, :].rearrange("(n p) d -> p n d", p=P)
                                 ).then_inc(y_loaded[b], 16)
            sorted_tiles(0)
            clear_sorted()

            def store_values(b):
                sp.wait_ge(val_copied, b + 1)
                sp.dma_start(vd[b, :, PAD:VROW], VS[:, :]).then_inc(val_stored, 16)
            for b in range(B):
                store_values(b)
            sp.wait_ge(val_stored, 16 * B)
            sp.wait_ge(w_loaded, WL)

            def load_values(b, hh, u):
                if not (isinstance(u, int) and u == 0):
                    sp.wait_ge(prod_done, 16 * u)
                else:
                    sp.wait_ge(down_done, SORTED)
                for j in range(OFFS):
                    row = 32 * (j % 4) + 8 * (j // 4)
                    first = PAD - VPAD - j
                    src = vd[b, hh * HH * HS:(hh + 1) * HH * HS, first:first + VW]
                    sp.dma_start(VSH[row:row + HH, :, :], src.rearrange("(h e) w -> h e w", e=HS)
                                 ).then_inc(vsh_loaded, 16)

            def store(b):
                sp.wait_ge(ffn_added, B + b + 1)
                sp.dma_start(out[b].rearrange("(n p) d -> p n d", p=P),
                             X[:, b * TB:(b + 1) * TB, :]).then_inc(out_stored, 16)
            for hh in range(HALVES):
                load_values(0, hh, hh)
            with sp.Fori(1, B) as b:
                for hh in range(HALVES):
                    load_values(b, hh, 2 * b + hh)
            sp.wait_ge(prod_done, 16 * (2 * B - 1) + HS)
            sp.wait_ge(dve_products, HS)
            sp.wait_ge(x_added, 4 * B)
            load_experts()
            sorted_tiles(1)
            for b in range(B):
                store(b)
            sp.wait_ge(out_stored, 16 * B)

        @block.gpsimd
        def _(pool):
            pool.memset(SPARE, 0.0).then_inc(spare_cleared, 1)
            pool.iota(IT[:, 0:1], [[0, 1]], base=0, channel_multiplier=1).then_inc(pool_const, 1)
            pool.iota(COLI[:, :], [[1, 128]], base=0, channel_multiplier=0).then_inc(pool_const, 1)
            pool.iota(COLHI[:, :], [[0, 16], [1, 8]], base=0, channel_multiplier=0).then_inc(pool_const, 1)
            pool.iota(COLBI[:, :], [[1, 8], [0, 16]], base=0, channel_multiplier=0).then_inc(pool_const, 1)
            pool.iota(CMI[:, :, :], [[-OFFS, GROUPS], [1, PAD]], base=0, channel_multiplier=0
                      ).then_inc(pool_const, 1)
            pool.wait_ge(spare_cleared, 1)
            pool.iota(SPAREN[:, :, D:D + 1].bitcast(i32), [[P, UNROLL]], base=B * T, channel_multiplier=1
                      ).then_inc(spare_ready, 1)

            def scatter(ph):
                pool.wait_ge(norm_ready, 2 * B * ph + 1)
                pool.iota(UID[:, :, D:D + 1].bitcast(i32), [[P, TILES]], base=0, channel_multiplier=1
                          ).then_inc(numbered, 1)
                pool.wait_ge(numbered, ph + 1)
                pool.wait_ge(route_ready, ph + 1)
                pool.wait_ge(xs_cleared, 16 * (ph + 1))
                for n in range(TILES):
                    pool.indirect_dma_start(
                        out=xs_d, out_offset=bass.IndirectOffsetOnAxis(POS[:, n:n + 1], 0),
                        in_=UID[:, n, :], in_offset=None).then_inc(scattered, 16)

            def outputs(ph):
                for t in range(SORTED):
                    pool.wait_ge(y_ready, SORTED * ph + t + 1)
                    pool.indirect_dma_start(
                        out=ys_d, out_offset=bass.IndirectOffsetOnAxis(XS[t % UNROLL][:, D:D + 1].bitcast(u32), 0),
                        in_=YB[t % 4], in_offset=None).then_inc(y_stored[t % 4], 16)
            scatter(0)
            outputs(0)

            def difference(u, g, p):
                n = 8 * g + p
                pool.wait_ge(pad_ready, 2 * u + 1)
                if not (isinstance(u, int) and u == 0 and n < RING):
                    pool.wait_ge(pe_used, 32 * u + (n - RING) // 2 + 1)
                j = OFFS * (g // 2) + 2 * p
                pool.tensor_tensor(A[n % RING][:, :, :], window(DPAD[:, PAD - j - 1:PAD - j], [[1, 2], [1, T]]),
                                   window(DPAD[:, PAD:PAD + 1], [[0, 2], [1, T]]), ALU.subtract
                                   ).then_inc(pool_args, 1)

            def product(v, hh, i):
                half, e = divmod(i, HS)
                first = VPAD + half * BANK
                if i == 0:
                    if isinstance(v, int) and v == 0:
                        pool.wait_ge(xs_cleared, 32)
                    pool.wait_ge(exp_done, v + 1)
                    pool.wait_ge(vsh_loaded, 16 * OFFS * (v + 1))
                if not (isinstance(v, int) and v == 0 and i < 2):
                    pool.wait_ge(num_used, 16 * v + i - 1)
                pool.tensor_tensor(Y[i % 2][:, :, :], LT[hh][:, :, half * BANK:(half + 1) * BANK],
                                   window(VSH[:, e, first:first + 1], [[-OFFS, GROUPS], [1, BANK]]),
                                   ALU.mult).then_inc(prod_done, 1)

            def unit(u, hh, v):
                made = 0
                for n, ahead in zip(POOL_SLOTS + (None,), PRODUCTS_AHEAD + (2 * HS,)):
                    if v is not None:
                        for i in range(made, ahead):
                            product(v, 1 - hh, i)
                        made = ahead
                    if n is not None:
                        difference(u, *divmod(n, PAIRS))
            unit(0, 0, None)
            unit(1, 1, 0)
            with pool.Fori(1, B) as b:
                for hh in range(HALVES):
                    unit(2 * b + hh, hh, 2 * b + hh - 1)
            for i in range(0, 2 * HS, 2):
                product(2 * B - 1, 1, i)
            scatter(1)
            outputs(1)

        @block.scalar
        def _(act):
            def squares(r, b):
                act.wait_ge(norm_centred, B * r + b + 1)
                act.activation(NSQ[b % 2], U[:, b * TB:(b + 1) * TB, :], ACT.Square).then_inc(norm_squares, 1)

            def roots(r, b):
                act.wait_ge(norm_args, B * r + b + 1)
                cols = slice(b * TB, (b + 1) * TB)
                act.activation(STAT[:, 5, cols], STAT[:, 2, cols], ACT.Sqrt).then_inc(norm_roots, 1)

            def norm(r, after):
                for b in range(B + 2):
                    if b < B:
                        squares(r, b)
                    if 1 <= b <= B:
                        roots(r, b - 1)
                    if b >= 2:
                        after(b - 2)

            def evacuate(ph, b):
                act.wait_ge(u_transposed, 2 * B * ph + b + 1)
                if b >= 2:
                    act.wait_ge(gate_logits, B * ph + b - 1)
                act.activation(UT[b % 2], ACC[b % 2][:, :], ACT.Copy).then_inc(u_evacuated, 1)

            def ffn(ph):
                act.wait_ge(gate_shifted, ph + 1)
                act.activation(GT[1], GT[0], ACT.Exp).then_inc(gate_exp, 1)

                def slot(i, c, held):
                    if inside(i, c + 1):
                        later(biased, act, ph, i, c + 1, 0)
                        later(h_turned, act, ph, i, c + 1, 2)
                        act.activation(HS_[(c + 1) % 2], HB[(c + 1) % 2], ACT.Silu).then_inc(silu_done, 1)
                    if inside(i, c):
                        later(h_turned, act, ph, i, c, 0)
                        later(down_done, act, ph, i, c, 2)
                        act.activation(HST[c % 2], ACC[0][:, (c % 2) * BANK:(c % 2 + 1) * BANK], ACT.Copy
                                       ).then_inc(ht_ready, 1)
                slots(act, slot)
            norm(0, lambda b: evacuate(0, b))
            ffn(0)
            act.wait_ge(consts_ready, 1)

            def tokens(b):
                act.wait_ge(u_transposed, B + b + 1)
                act.activation(YT[:, b * T:(b + 1) * T], ACC[b % 2][:, :], ACT.Copy).then_inc(yt_ready, 1)
            norm(1, tokens)

            def values(b):
                act.wait_ge(val_done, b + 1)
                if b > 0:
                    act.wait_ge(val_stored, 16 * b)
                for half in range(NB):
                    last = act.activation(VS[:, half * BANK:(half + 1) * BANK], MX[half][:, :], ACT.Copy)
                last.then_inc(val_copied, 1)

            def gelu(u, g, p):
                n = 8 * g + p
                by_pool = sum(1 for s in POOL_SLOTS if s < n)
                if n in POOL_SLOTS:
                    act.wait_ge(pool_args, PA * u + by_pool + 1)
                else:
                    act.wait_ge(dve_args, DA * u + n - by_pool + 1)
                bias = BDMG[:, :] if g % 2 == 0 else 0.0
                act.activation(A[n % RING][:, :, :], A[n % RING][:, :, :], ACT.Gelu, bias=bias
                               ).then_inc(gelu_done, 1)

            def damage(u, hh, g):
                act.wait_ge(pe_used, 4 * (8 * u + g + 1))
                act.activation(LT[hh][:, g // 2, :], SUMS[:, :], ACT.Tanh, bias=BOUTH[:, :], scale=0.5
                               ).then_inc(tanh_done, 1)

            def logits(u, hh, g):
                act.wait_ge(pe_used, 4 * (8 * u + g + 1))
                act.activation(LT[hh][:, g // 2, :], SUMS[:, :], ACT.Copy).then_inc(bond_evac, 1)

            def exponentials(v, hh):
                act.wait_ge(shifted, 2 * v + 2)
                act.activation(LT[hh][:, :, :], LT[hh][:, :, :], ACT.Exp).then_inc(exp_done, 1)

            def spread_reciprocals(v):
                act.wait_ge(recip_done, v + 1)
                act.activation(SPREAD, R8[:, :, :].unsqueeze(2).broadcast_to([P, TB, OFFS, HH]), ACT.Copy
                               ).then_inc(recip_spread, 1)

            def reciprocals(v, half):
                act.wait_ge(rbc_done, 2 * v + half + 1)
                if half == 0 and not (isinstance(v, int) and v == 0):
                    act.wait_ge(norm_done, 2 * v)
                act.activation(RD[:, half * BANK:(half + 1) * BANK], MX[1][:, :], ACT.Copy).then_inc(rd_ready, 1)

            def unit(u, hh, v):
                for g in range(2 * GROUPS):
                    for p in range(PAIRS):
                        if v is not None and 8 * g + p == EXP_AT:
                            exponentials(v, 1 - hh)
                        if v is not None and 8 * g + p == SPREAD_AT:
                            spread_reciprocals(v)
                        if v is not None and 8 * g + p in RD_AT:
                            reciprocals(v, RD_AT.index(8 * g + p))
                        if p == 2 and g % 2 == 1:
                            damage(u, hh, g - 1)
                        if p == 2 and g % 2 == 0 and g > 0:
                            logits(u, hh, g - 1)
                        if p == 2 and g == 0 and v is not None:
                            logits(v, 1 - hh, 2 * GROUPS - 1)
                        if v is None and p == 2 and g % 2 == 0:
                            values(g // 2)
                        gelu(u, g, p)
            unit(0, 0, None)
            unit(1, 1, 0)
            with act.Fori(1, B) as b:
                for hh in range(HALVES):
                    unit(2 * b + hh, hh, 2 * b + hh - 1)
            logits(2 * B - 1, 1, 2 * GROUPS - 1)
            for b in range(B - 1):
                squares(2, b)
                if b > 0:
                    roots(2, b - 1)
            roots(2, B - 2)
            exponentials(2 * B - 1, 1)
            spread_reciprocals(2 * B - 1)
            for half in range(2):
                reciprocals(2 * B - 1, half)
            for b in range(B - 1):
                evacuate(1, b)
            squares(2, B - 1)
            roots(2, B - 1)
            evacuate(1, B - 1)
            ffn(1)

        @block.vector
        def _(dve):
            dve.memset(WC[:, :, :], 0.0).then_inc(dve_const, 1)
            dve.memset(ZP[:, :], 0.0).then_inc(dve_const, 1)
            dve.memset(TRI[:, :], 0.0).then_inc(dve_const, 1)
            done = [3]

            def step(ins):
                ins.then_inc(dve_const, 1)
                done[0] += 1
                dve.wait_ge(dve_const, done[0])

            step(dve.memset(ONES[:, :], 1.0))
            dve.wait_ge(pool_const, 5)
            step(dve.tensor_copy(ITF[:, 3:4], IT[:, 0:1]))
            step(dve.tensor_copy(COL[:, :], COLI))
            step(dve.tensor_scalar(TRI[:, :], COL[:, :], ITF[:, 3:4], None, ALU.is_gt))
            dve.tensor_scalar(IDENT[:, :], COL[:, :], ITF[:, 3:4], None, ALU.is_equal).then_inc(consts_ffn, 1)
            dve.wait_ge(consts_ffn, 1)
            dve.wait_ge(pe_const, 1)
            dve.tensor_copy(COLS[:, :], MX[0][:, 0:E + 1]).then_inc(weights_ready, 1)
            dve.wait_ge(weights_ready, 1)
            dve.tensor_scalar(GATEW[:, :], COLS[:, 0:E], COLS[:, E:E + 1], None, ALU.mult
                              ).then_inc(weights_ready, 1)

            def attention_constants():
                dve.wait_ge(w_loaded, WL)
                step(dve.tensor_scalar(MINUS5[:, :], IDENT[:, :], -5.0, None, ALU.mult))
                step(dve.tensor_scalar(BOUTH[:, :], BOUT[:, :], 0.5, None, ALU.mult))
                step(dve.memset(DPAD[:, 0:PAD], 0.0))
                step(dve.memset(SPAD[:, 0:PAD], 0.0))
                step(dve.tensor_scalar(IT[:, 1:2], IT[:, 0:1], 5, None, ALU.logical_shift_right))
                step(dve.tensor_scalar(IT[:, 2:3], IT[:, 0:1], 3, 3, ALU.logical_shift_right, ALU.bitwise_and))
                step(dve.tensor_scalar(ITF[:, 0:1], IT[:, 2:3], 4.0, None, ALU.mult))
                step(dve.tensor_copy(ITF[:, 1:2], IT[:, 1:2]))
                step(dve.tensor_tensor(ITF[:, 0:1], ITF[:, 0:1], ITF[:, 1:2], ALU.add))
                step(dve.tensor_scalar(IT[:, 3:4], IT[:, 0:1], 7, None, ALU.bitwise_and))
                step(dve.tensor_copy(ITF[:, 1:2], IT[:, 3:4]))
                step(dve.tensor_scalar(IT[:, 3:4], IT[:, 0:1], 4, None, ALU.logical_shift_right))
                step(dve.tensor_copy(ITF[:, 2:3], IT[:, 3:4]))
                step(dve.tensor_copy(COLH[:, :], COLHI[:, :]))
                step(dve.tensor_copy(COLB[:, :], COLBI[:, :]))
                step(dve.tensor_copy(CMASK[:, :, :], CMI[:, :, :]))
                step(dve.tensor_scalar(CMASK[:, :, :], CMASK[:, :, :], ITF[:, 0:1], -1e30, ALU.is_lt, ALU.mult))
                step(dve.tensor_scalar(SELALL[:, :], COLH[:, :], ITF[:, 1:2], None, ALU.is_equal))
                for par in range(2):
                    step(dve.tensor_scalar(SELE[:, par, :], COL[:, 0:32], -8.0 * par, ITF[:, 1:2], ALU.add,
                                           ALU.is_equal))
                for kind in range(2):
                    for k in range(4):
                        step(dve.tensor_scalar(WSEL[:, kind, k, :], COL[:, 0:32], -8.0 * k, ITF[:, 2:3],
                                               ALU.add, ALU.is_equal))
                        step(dve.tensor_scalar(WSEL[:, kind, k, :], WSEL[:, kind, k, :], WCOL[:, kind:kind + 1],
                                               None, ALU.mult))
                step(dve.tensor_scalar(COLB[:, :], COLB[:, :], ITF[:, 2:3], None, ALU.is_equal))
                for kind in range(2):
                    step(dve.tensor_tensor(BDW[:, kind, :].rearrange("p (h c) -> p h c", c=BD),
                                           COLB[:, :].rearrange("p (h c) -> p h c", c=BD),
                                           WREP[:, kind, :].unsqueeze(1).broadcast_to([P, HH, BD]), ALU.mult))
                dve.tensor_copy(WPOSR[:, :, :], WPOS[:, :].unsqueeze(1).broadcast_to([BD, HH, BD])
                                ).then_inc(consts_ready, 1)
                dve.wait_ge(pe_const, 2)
                dve.tensor_copy(RELT[:, :], MX[0][0:BD, 0:HORIZON]).then_inc(weights_ready, 1)
                dve.wait_ge(pe_const, 3)
                dve.tensor_copy(WDT[:, :, :].rearrange("p h c -> p (h c)"), MX[1][:, 0:HALVES * P]
                                ).then_inc(weights_ready, 1)
                dve.wait_ge(pe_const, 4)
                dve.tensor_copy(PCOL[:, :], MX[0][:, 0:HORIZON]).then_inc(weights_ready, 1)
                dve.wait_ge(pe_const, 5)
                dve.tensor_copy(F[:, :, :, :].rearrange("p h k c -> p (h k c)"), MX[1][:, :]
                                ).then_inc(weights_ready, 1)

            def wide(row, b):
                return STAT[:, row, b * TB:(b + 1) * TB].unsqueeze(2).broadcast_to([P, TB, D])

            def norm(r, rms, arrive):
                for b in range(B + 1):
                    if b < B:
                        arrive(b)
                        norm_centre(r, b)
                    if b > 0:
                        norm_scale(r, b - 1, rms)

            def norm_centre(r, b):
                tiles = slice(b * TB, (b + 1) * TB)
                n = B * r + b + 1
                dve.tensor_reduce(STAT[:, 0, tiles], X[:, tiles, :], AX.X, ALU.add).then_inc(norm_sums, 1)
                dve.wait_ge(norm_sums, n)
                dve.tensor_scalar(STAT[:, 1, tiles], STAT[:, 0, tiles], 1.0 / D, None, ALU.mult
                                  ).then_inc(norm_means, 1)
                dve.wait_ge(norm_means, n)
                dve.tensor_tensor(U[:, tiles, :], X[:, tiles, :], wide(1, b), ALU.subtract
                                  ).then_inc(norm_centred, 1)

            def norm_scale(r, b, rms):
                tiles = slice(b * TB, (b + 1) * TB)
                n = B * r + b + 1
                dve.wait_ge(norm_squares, n)
                dve.tensor_reduce(STAT[:, 4, tiles], NSQ[b % 2], AX.X, ALU.add).then_inc(norm_vars, 1)
                dve.wait_ge(norm_vars, n)
                slope, base = (1.0 + RMS_EPS, RMS_EPS * LN_EPS) if rms else (1.0, LN_EPS)
                arg, y, w = STAT[:, 2, tiles], STAT[:, 3, tiles], STAT[:, 0, tiles]
                dve.tensor_scalar(arg, STAT[:, 4, tiles], slope / D, base, ALU.mult, ALU.add
                                  ).then_inc(norm_args, 1)
                dve.wait_ge(norm_roots, n)
                k = 5 * (n - 1)
                dve.reciprocal(y, STAT[:, 5, tiles]).then_inc(norm_newton, 1)
                dve.wait_ge(norm_newton, k + 1)
                dve.tensor_tensor(w, y, y, ALU.mult).then_inc(norm_newton, 1)
                dve.wait_ge(norm_newton, k + 2)
                dve.tensor_tensor(w, w, arg, ALU.mult).then_inc(norm_newton, 1)
                dve.wait_ge(norm_newton, k + 3)
                dve.tensor_scalar(w, w, -0.5, 1.5, ALU.mult, ALU.add).then_inc(norm_newton, 1)
                dve.wait_ge(norm_newton, k + 4)
                dve.tensor_tensor(y, y, w, ALU.mult).then_inc(norm_newton, 1)
                dve.wait_ge(norm_newton, k + 5)
                dve.tensor_tensor(U[:, tiles, :], U[:, tiles, :], wide(3, b), ALU.mult).then_inc(norm_ready, 1)

            routed = [0]

            def rstep(ins):
                ins.then_inc(route_steps, 1)
                routed[0] += 1
                dve.wait_ge(route_steps, routed[0])

            def spread(table):
                return table.unsqueeze(2).broadcast_to([P, TILES, E])

            def route(ph):
                dve.wait_ge(gate_logits, B * (ph + 1))
                lg = CT[:, 0:TILES * E].rearrange("p (n e) -> p n e", e=E)
                rstep(dve.tensor_reduce(STAT[:, 0, :], lg, AX.X, ALU.max))
                dve.tensor_tensor(GT[0], lg, spread(STAT[:, 0, :]), ALU.subtract).then_inc(gate_shifted, 1)
                dve.wait_ge(gate_shifted, ph + 1)
                rstep(dve.tensor_scalar(GT[2], GT[0], 0.0, -16.0, ALU.is_ge, ALU.mult))
                rstep(dve.tensor_tensor(GT[2], GT[2], COL[:, 0:E].unsqueeze(1).broadcast_to([P, TILES, E]),
                                        ALU.add))
                rstep(dve.tensor_reduce(STAT[:, 1, :], GT[2], AX.X, ALU.min))
                dve.tensor_tensor(GT[3], GT[2], spread(STAT[:, 1, :]), ALU.is_equal).then_inc(onehot_ready, 1)
                dve.wait_ge(onehot_ready, ph + 1)
                dve.wait_ge(gate_exp, ph + 1)
                rstep(dve.tensor_reduce(STAT[:, 2, :], GT[1], AX.X, ALU.add))
                rstep(dve.reciprocal(STAT[:, 3, :], STAT[:, 2, :]))
                rstep(dve.tensor_scalar(SCORE[:, :], STAT[:, 3, :], 0.5, None, ALU.mult))
                dve.wait_ge(ranks_done, ph + 1)
                before = MX[1][:, 0:TILES * E].rearrange("p (n e) -> p n e", e=E)
                rstep(dve.tensor_copy(GT[4], MX[1][:, TILES * E:2 * TILES * E].rearrange(
                    "p (n e) -> p n e", e=E)))
                src, dst, reach = 4, 5, 1
                while reach < TILES:
                    dve.tensor_copy(GT[dst][:, 0:reach, :], GT[src][:, 0:reach, :])
                    rstep(dve.tensor_tensor(GT[dst][:, reach:TILES, :], GT[src][:, reach:TILES, :],
                                            GT[src][:, 0:TILES - reach, :], ALU.add))
                    src, dst, reach = dst, (6 if dst == 5 else 5), 2 * reach
                total = GT[src][:, TILES - 1, :]
                rstep(dve.tensor_scalar(CNTI[:, :], total, float(P - 1), None, ALU.add))
                rstep(dve.tensor_scalar(CNTI[:, :], CNTI[:, :], P.bit_length() - 1, None,
                                        ALU.logical_shift_right))
                rstep(dve.tensor_copy(SMALL[:, 0, :], CNTI[:, :]))
                last, reach = 0, 1
                while reach < E:
                    dve.tensor_copy(SMALL[:, last + 1, 0:reach], SMALL[:, last, 0:reach])
                    rstep(dve.tensor_tensor(SMALL[:, last + 1, reach:E], SMALL[:, last, reach:E],
                                            SMALL[:, last, 0:E - reach], ALU.add))
                    last, reach = last + 1, 2 * reach
                ends = SMALL[:, last, :]
                rstep(dve.tensor_tensor(SMALL[:, 4, :], ends, SMALL[:, 0, :], ALU.subtract))
                rstep(dve.tensor_scalar(SMALL[:, 5, :], SMALL[:, 4, :], float(P), None, ALU.mult))
                rstep(dve.tensor_tensor(GT[7], GT[src], GT[4], ALU.subtract))
                rstep(dve.tensor_tensor(GT[7], GT[7], before, ALU.add))
                rstep(dve.tensor_tensor(GT[7], GT[7], SMALL[:, 5, :].unsqueeze(1).broadcast_to([P, TILES, E]),
                                        ALU.add))
                rstep(dve.tensor_tensor(GT[7], GT[7], GT[3], ALU.mult))
                rstep(dve.tensor_reduce(STAT[:, 0, :], GT[7], AX.X, ALU.add))
                dve.tensor_copy(POS[:, :], STAT[:, 0, :]).then_inc(route_ready, 1)
                marks = AF[2][:, 0:SORTED * E].rearrange("p (k e) -> p k e", e=E)
                rstep(dve.tensor_tensor(marks, COL[:, 0:SORTED].unsqueeze(2).broadcast_to([P, SORTED, E]),
                                        ends.unsqueeze(1).broadcast_to([P, SORTED, E]), ALU.is_ge))
                rstep(dve.tensor_reduce(EIDF[:, :], marks, AX.X, ALU.add))
                dve.tensor_scalar(EID[:, :], EIDF[:, :], float(E - 1), None, ALU.min).then_inc(eid_ready, 1)
                dve.wait_ge(eid_ready, ph + 1)

            def experts(ph):
                dve.wait_ge(ffn_loaded, 16 * (E + 3) * (ph + 1))

                def slot(i, c, held):
                    e_up, e_down = experts_of(dve, i, c, held)
                    if inside(i, c + 2):
                        k = (c + 2) % 2
                        later(x_turned, dve, ph, i, c + 2, 0)
                        later(up_done, dve, ph, i, c + 2, 2)
                        dve.tensor_scalar(XST[k], MX[k][:, 0:P], COLS[:, E:E + 1], None, ALU.mult
                                          ).then_inc(xt_ready, 1)
                    if inside(i, c + 1):
                        k = (c + 1) % 2
                        later(up_done, dve, ph, i, c + 1, 0)
                        later(silu_done, dve, ph, i, c + 1, 2)
                        dve.tensor_tensor(HB[k], CT[:, k * BANK:(k + 1) * BANK], B1S[:, bass.ds(e_up * FF, FF)],
                                          ALU.add).then_inc(biased, 1)
                    if inside(i, c - 1):
                        k = (c - 1) % 4
                        later(down_done, dve, ph, i, c - 1, 0)
                        if ph > 0 or not isinstance(i, int) or UNROLL * i + c - 5 >= 0:
                            dve.wait_ge(y_stored[k], 16 * ((SORTED // 4) * ph + 2 * i + (c - 1) // 4))
                        at = ((c - 1) % 2) * BANK
                        dve.tensor_tensor(YB[k], ACC[1][:, at:at + D], B2S[:, bass.ds(e_down * D, D)],
                                          ALU.add).then_inc(y_ready, 1)
                slots(dve, slot)

            def add_outputs(ph, b):
                dve.wait_ge(y_loaded[b], 16 * (ph + 1))
                for n in range(b * TB, (b + 1) * TB):
                    last = dve.scalar_tensor_tensor(X[:, n, :], YG[:, n, :], SCORE[:, n:n + 1], X[:, n, :],
                                                    ALU.mult, ALU.add)
                last.then_inc(ffn_added, 1)
                dve.wait_ge(ffn_added, B * ph + b + 1)

            norm(0, True, lambda b: dve.wait_ge(x_loaded[b], 16))
            route(0)
            attention_constants()
            experts(0)
            norm(1, False, lambda b: add_outputs(0, b))

            def copy_pad(u, kind):
                dve.wait_ge(ct_ready, 2 * u + kind + 1)
                if kind == 0 and not (isinstance(u, int) and u == 0):
                    dve.wait_ge(pool_args, PA * u)
                dve.tensor_copy((DPAD, SPAD)[kind][:, PAD:PAD + T], PROJ[kind][:, :]).then_inc(pad_ready, 1)
                dve.wait_ge(pad_ready, 2 * u + kind + 1)

            def difference(u, g, p):
                n = 8 * g + p
                if not (isinstance(u, int) and u == 0 and n < RING):
                    dve.wait_ge(pe_used, 32 * u + (n - RING) // 2 + 1)
                slot = A[n % RING]
                j = OFFS * (g // 2) + 2 * p
                if g % 2 == 0:
                    dve.tensor_tensor(slot[:, :, :], window(DPAD[:, PAD - j - 1:PAD - j], [[1, 2], [1, T]]),
                                      window(PROJ[0][:, 0:1], [[0, 2], [1, T]]), ALU.subtract).then_inc(dve_args, 1)
                else:
                    for i in range(2):
                        ji = j + 1 - i
                        last = dve.scalar_tensor_tensor(
                            slot[:, i, :], SPAD[:, PAD - ji:PAD - ji + T],
                            PCOL[:, HORIZON - 1 - ji:HORIZON - ji], PROJ[1][:, :], ALU.add, ALU.subtract)
                    last.then_inc(dve_args, 1)

            def tail(v, vb, hh, s):
                lt = LT[hh]
                if s == 4:
                    dve.wait_ge(bond_evac, 4 * v + 4)
                    dve.tensor_tensor(lt[:, :, 0:PAD], lt[:, :, 0:PAD], CMASK[:, :, :], ALU.add
                                      ).then_inc(masked, 1)
                if 7 <= s <= 10:
                    for tb in (2 * (s - 7), 2 * (s - 7) + 1):
                        dve.wait_ge(transposed, TB * v + tb + 1)
                        dve.tensor_reduce(M8[:, tb, :], MX[tb % 2][:, :].rearrange("p (j h) -> p h j", h=HH),
                                          AX.X, ALU.max).then_inc(max_done, 1)
                if s == SHIFT_AT:
                    for half in range(2):
                        dve.wait_ge(mbc_done, 2 * v + half + 1)
                        cols = slice(half * BANK, (half + 1) * BANK)
                        dve.tensor_tensor(lt[:, :, cols], lt[:, :, cols],
                                          window(MX[half][:, 0:1], [[0, GROUPS], [1, BANK]]), ALU.subtract
                                          ).then_inc(shifted, 1)
                if s == 10:
                    dve.wait_ge(max_done, TB * (v + 1))
                    if not (isinstance(v, int) and v == 0):
                        dve.wait_ge(cproj_done, 2 * v)
                    dve.tensor_copy(SPREAD, M8[:, :, :].unsqueeze(2).broadcast_to([P, TB, OFFS, HH])
                                    ).then_inc(max_spread, 1)
                if s == 21:
                    dve.wait_ge(den_done, 4 * (v + 1))
                    dve.reciprocal(R8[:, :, :].rearrange("p n h -> p (n h)"), MX[1][:, 0:TB * HH]
                                   ).then_inc(recip_done, 1)
                if s in (25, 33):
                    half = (s - 25) // 8
                    cols = slice(half * BANK, (half + 1) * BANK)
                    dve.wait_ge(num_used, 16 * v + 8 * (half + 1))
                    dve.wait_ge(rd_ready, 2 * v + half + 1)
                    if half == 0:
                        if not (isinstance(v, int) and v == 0):
                            dve.wait_ge(cproj_done, 2 * v)
                    dve.tensor_tensor(O[:, cols], MX[0][:, :], RD[:, cols], ALU.mult).then_inc(norm_done, 1)
                if s in (31, 36):
                    half = (s - 31) // 5
                    dve.wait_ge(cproj_done, 2 * v + half + 1)
                    first = vb * TB + half * TB // 2
                    xs = X[:, bass.ds(first, TB // 2), :]
                    dve.tensor_tensor(xs, xs, MX[1][:, :].rearrange("p (n d) -> p n d", d=D), ALU.add
                                      ).then_inc(x_added, 1)

            def product(i):
                v = 2 * B - 1
                half, e = divmod(i, HS)
                first = VPAD + half * BANK
                dve.wait_ge(exp_done, v + 1)
                dve.wait_ge(vsh_loaded, 16 * OFFS * (v + 1))
                dve.wait_ge(num_used, 16 * v + i - 1)
                dve.tensor_tensor(Y[i % 2][:, :, :], LT[1][:, :, half * BANK:(half + 1) * BANK],
                                  window(VSH[:, e, first:first + 1], [[-OFFS, GROUPS], [1, BANK]]),
                                  ALU.mult).then_inc(dve_products, 1)

            def unit(u, hh, v, vb, v2, vb2):
                copy_pad(u, 0)
                for g in range(2 * GROUPS):
                    if g == 1:
                        copy_pad(u, 1)
                    for p in range(PAIRS):
                        if PAIRS * g + p not in POOL_SLOTS:
                            difference(u, g, p)
                        if p % 2 == 1:
                            s = 4 * g + p // 2
                            if s < 5 and v2 is not None:
                                tail(v2, vb2, hh, STEPS + s)
                            if v is not None:
                                tail(v, vb, 1 - hh, s)

            unit(0, 0, None, None, None, None)
            unit(1, 1, 0, 0, None, None)
            with dve.Fori(1, B) as b:
                unit(2 * b, 0, 2 * b - 1, b - 1, 2 * b - 2, b - 1)
                unit(2 * b + 1, 1, 2 * b, b, 2 * b - 1, b - 1)
            for s in range(STEPS, STEPS + 5):
                tail(2 * B - 2, B - 1, 0, s)
            PRODUCT_STEPS = (17, 20, 21, 22, 24, 26, 27, 28)
            for s in range(STEPS + 5):
                tail(2 * B - 1, B - 1, 1, s)
                if s == 4:
                    dve.wait_ge(x_added, 4 * B - 2)
                    for b in range(B):
                        if b < B - 1:
                            norm_centre(2, b)
                        if b > 0:
                            norm_scale(2, b - 1, True)
                if s in PRODUCT_STEPS:
                    product(2 * PRODUCT_STEPS.index(s) + 1)
            dve.wait_ge(x_added, 4 * B)
            norm_centre(2, B - 1)
            norm_scale(2, B - 1, True)
            route(1)
            experts(1)
            for b in range(B):
                add_outputs(1, b)

        @block.tensor
        def _(pe):
            pe.wait_ge(consts_ffn, 1)
            pe.wait_ge(rows_loaded, 32)
            pe.transpose(MX[0][:, 0:E + 1], ROWS[:, :], IDENT[0:E + 1, 0:E + 1]).then_inc(pe_const, 1)
            pe.wait_ge(weights_ready, 2)

            def attention_constants():
                pe.wait_ge(consts_ready, 1)
                pe.wait_ge(w_loaded, WL)
                pe.transpose(MX[0][0:BD, 0:HORIZON], REL[:, :], IDENT[0:HORIZON, 0:HORIZON]).then_inc(pe_const, 1)
                for hh in range(HALVES):
                    last = pe.transpose(MX[1][:, hh * P:(hh + 1) * P], WDISP[:, hh * P:(hh + 1) * P], IDENT[:, :])
                last.then_inc(pe_const, 1)
                pe.wait_ge(weights_ready, 4)
                pe.matmul(MX[0][:, 0:HORIZON], WPOSR[:, :, :].rearrange("p h c -> p (h c)"), RELT[:, :],
                          start=True, stop=True).then_inc(pe_const, 1)
                for hh in range(HALVES):
                    for kind in range(2):
                        col = (2 * hh + kind) * P
                        last = pe.matmul(MX[1][:, col:col + P], WDT[:, hh, :], BDW[:, 1 - kind, :],
                                         start=True, stop=True)
                last.then_inc(pe_const, 1)
                pe.wait_ge(weights_ready, 6)

            def turn(r, b):
                pe.wait_ge(norm_ready, B * r + b + 1)
                for n in range(TB):
                    last = pe.transpose(ACC[b % 2][:, n * P:(n + 1) * P], U[:, b * TB + n, :], IDENT[:, :])
                last.then_inc(u_transposed, 1)

            def gate(ph, b):
                if b >= 2:
                    pe.wait_ge(u_evacuated, B * ph + b - 1)
                turn(2 * ph, b)
                pe.wait_ge(u_evacuated, B * ph + b + 1)
                for n in range(TB):
                    at = (b * TB + n) * E
                    last = pe.matmul(CT[:, at:at + E], UT[b % 2][:, n * P:(n + 1) * P], GATEW[:, :],
                                     start=True, stop=True)
                last.then_inc(gate_logits, 1)

            def ffn(ph):
                pe.wait_ge(onehot_ready, ph + 1)
                onehot = GT[3].rearrange("p n e -> p (n e)")
                pe.matmul(MX[1][:, 0:TILES * E], TRI[:, :], onehot, start=True, stop=True)
                pe.matmul(MX[1][:, TILES * E:2 * TILES * E], ONES[:, :], onehot, start=True, stop=True
                          ).then_inc(ranks_done, 1)
                pe.wait_ge(eid_ready, ph + 1)
                if ph == 0:
                    attention_constants()
                pe.wait_ge(ffn_loaded, 16 * (E + 3) * (ph + 1))

                def slot(i, c, held):
                    e_up, e_down = experts_of(pe, i, c, held)
                    if inside(i, c + 2):
                        k = (c + 2) % 2
                        pe.wait_ge(x_arrived[(c + 2) % UNROLL],
                                   16 * ((SORTED // UNROLL) * ph + i + (c + 2) // UNROLL + 1))
                        later(xt_ready, pe, ph, i, c + 2, 2)
                        pe.transpose(MX[k][:, 0:P], XS[(c + 2) % UNROLL][:, 0:D], IDENT[:, :]).then_inc(x_turned, 1)
                    if inside(i, c + 1):
                        k = (c + 1) % 2
                        later(xt_ready, pe, ph, i, c + 1, 0)
                        later(biased, pe, ph, i, c + 1, 2)
                        pe.matmul(CT[:, k * BANK:(k + 1) * BANK], XST[k], WFF[:, bass.ds(e_up * FF, FF)],
                                  start=True, stop=True).then_inc(up_done, 1)
                    if inside(i, c):
                        k = c % 2
                        later(silu_done, pe, ph, i, c, 0)
                        later(ht_ready, pe, ph, i, c, 2)
                        for f in range(FC):
                            at = k * BANK + f * P
                            last = pe.transpose(ACC[0][:, at:at + P], HS_[k][:, f * P:(f + 1) * P], IDENT[:, :])
                        last.then_inc(h_turned, 1)
                    if inside(i, c - 1):
                        k = (c - 1) % 2
                        later(ht_ready, pe, ph, i, c - 1, 0)
                        later(y_ready, pe, ph, i, c - 1, 2)
                        for f in range(FC):
                            last = pe.matmul(ACC[1][:, k * BANK:k * BANK + D], HST[k][:, f * P:(f + 1) * P],
                                             WFF[:, bass.ds(W2AT + e_down * FF + f * D, D)],
                                             start=(f == 0), stop=(f == FC - 1))
                        last.then_inc(down_done, 1)
                slots(pe, slot)

            for b in range(B):
                gate(0, b)
            ffn(0)
            for b in range(B):
                if b >= 2:
                    pe.wait_ge(yt_ready, b - 1)
                turn(1, b)
            pe.wait_ge(yt_ready, B)

            def values(b):
                if b > 0:
                    pe.wait_ge(val_copied, b)
                for half in range(NB):
                    last = pe.matmul(MX[half][:, :], WVAL[:, :],
                                     YT[:, b * T + half * BANK:b * T + (half + 1) * BANK], start=True, stop=True)
                last.then_inc(val_done, 1)

            def project(u, b, hh, kind):
                if not (isinstance(u, int) and u == 0):
                    pe.wait_ge(dve_args, DA * u - (PAIRS if kind == 0 else 0))
                for half in range(NB):
                    last = pe.matmul(PROJ[kind][:, half * BANK:(half + 1) * BANK], F[:, hh, kind, :],
                                     YT[:, bass.ds(b * T + half * BANK, BANK)], start=True, stop=True)
                last.then_inc(ct_ready, 1)

            def reduce(u, hh, s):
                g, k = divmod(s, 4)
                if k == 0:
                    if g % 2 == 1:
                        pe.wait_ge(tanh_done, 4 * u + g // 2 + 1)
                    elif g > 0 or not (isinstance(u, int) and u == 0):
                        pe.wait_ge(bond_evac, 4 * u + g // 2)
                pe.wait_ge(gelu_done, 64 * u + 2 * s + 2)
                kind = 1 - g % 2
                for half in range(NB):
                    for q in range(4):
                        slot = A[(2 * s + q // 2) % RING]
                        last = pe.matmul(SUMS[32 * q:32 * q + 32, half * BANK:(half + 1) * BANK],
                                         WSEL[:, kind, k, :],
                                         slot[:, 1 - q % 2, half * BANK:(half + 1) * BANK],
                                         start=(k == 0), stop=(k == 3 and kind == 1), tile_position=(0, 32 * q))
                if k == 3 and kind == 0:
                    for half in range(NB):
                        cols = slice(half * BANK, (half + 1) * BANK)
                        last = pe.matmul(SUMS[:, cols], MINUS5[:, :], LT[hh][:, g // 2, cols],
                                         start=False, stop=True)
                last.then_inc(pe_used, 1)

            def on_rows(to, half):
                for i in range(TB // 2):
                    last = pe.matmul(to[:, i * P:(i + 1) * P],
                                     SPREAD[:, half * TB // 2 + i, :, :].rearrange("p j h -> p (j h)"),
                                     IDENT[:, :], start=True, stop=True)
                return last

            def tail(v, hh, s):
                lt = LT[hh]
                first = isinstance(v, int) and v == 0
                if s == 5:
                    pe.wait_ge(masked, v + 1)
                if 5 <= s <= 8:
                    for tb in (2 * (s - 5), 2 * (s - 5) + 1):
                        if tb == 1 and not first:
                            pe.wait_ge(x_added, 2 * v)
                        if tb >= 2:
                            pe.wait_ge(max_done, TB * v + tb - 1)
                        for jg in range(GROUPS):
                            last = pe.transpose(MX[tb % 2][:, jg * P:(jg + 1) * P],
                                                lt[:, jg, tb * P:(tb + 1) * P], IDENT[:, :])
                        last.then_inc(transposed, 1)
                if s == 10:
                    pe.wait_ge(max_spread, v + 1)
                    for half in range(2):
                        on_rows(MX[half], half).then_inc(mbc_done, 1)
                if 15 <= s <= 18:
                    if s == 15:
                        pe.wait_ge(exp_done, v + 1)
                    for tb in (2 * (s - 15), 2 * (s - 15) + 1):
                        for jg in range(GROUPS):
                            last = pe.matmul(MX[1][:, tb * HH:(tb + 1) * HH], lt[:, jg, tb * P:(tb + 1) * P],
                                             SELALL[:, 0:HH], start=(jg == 0), stop=(jg == GROUPS - 1))
                    last.then_inc(den_done, 1)
                if s in (22, 24):
                    half = (s - 22) // 2
                    if half == 0:
                        pe.wait_ge(recip_spread, v + 1)
                    else:
                        pe.wait_ge(rd_ready, 2 * v + 1)
                    on_rows(MX[1], half).then_inc(rbc_done, 1)
                i = s - 15 if 15 <= s <= 22 else s - 16 if 24 <= s <= 31 else None
                if i is not None:
                    half, e = divmod(i, HS)
                    if not (isinstance(v, int) and v == 2 * B - 1):
                        pe.wait_ge(prod_done, 16 * v + i + 1)
                    elif i % 2:
                        pe.wait_ge(dve_products, i // 2 + 1)
                    else:
                        pe.wait_ge(prod_done, 16 * v + i // 2 + 1)
                    if i == HS:
                        pe.wait_ge(norm_done, 2 * v + 1)
                    q = e // 2
                    for jg in range(GROUPS):
                        last = pe.matmul(MX[0][32 * q:32 * q + 32, :], SELE[:, e % 2, :], Y[i % 2][:, jg, :],
                                         start=(e % 2 == 0 and jg == 0), stop=(e % 2 == 1 and jg == GROUPS - 1),
                                         tile_position=(0, 32 * q))
                    last.then_inc(num_used, 1)
                if s in (27, 34):
                    half = (s - 27) // 7
                    pe.wait_ge(norm_done, 2 * v + half + 1)
                    pe.wait_ge(rd_ready, 2 * v + 2)
                    if half:
                        pe.wait_ge(x_added, 2 * v + 1)
                    for i in range(TB // 2):
                        tok = (half * TB // 2 + i) * P
                        last = pe.matmul(MX[1][:, i * P:(i + 1) * P], O[:, tok:tok + P], WC[:, hh, :],
                                         start=True, stop=True)
                    last.then_inc(cproj_done, 1)

            def unit(u, b, hh, v, v2, nxt):
                for s in range(STEPS):
                    if s == 0:
                        project(u, b, hh, 1)
                    if s == STEPS - 4 and nxt is not None:
                        project(u + 1, nxt, 1 - hh, 0)
                    if v2 is not None and s < 3:
                        tail(v2, hh, STEPS + s)
                    if v is not None:
                        tail(v, 1 - hh, s)
                    elif s % 8 == 0:
                        values(s // 8)
                    reduce(u, hh, s)
            project(0, 0, 0, 0)
            unit(0, 0, 0, None, None, 0)
            pe.wait_ge(val_copied, B)
            unit(1, 0, 1, 0, None, 1)
            with pe.Fori(1, B - 1) as b:
                unit(2 * b, b, 0, 2 * b - 1, 2 * b - 2, b)
                unit(2 * b + 1, b, 1, 2 * b, 2 * b - 1, b + 1)
            unit(2 * B - 2, B - 1, 0, 2 * B - 3, 2 * B - 4, B - 1)
            unit(2 * B - 1, B - 1, 1, 2 * B - 2, 2 * B - 3, None)
            for s in range(STEPS, STEPS + 3):
                tail(2 * B - 2, 0, s)
            GATE_STEPS = (25, 27, 29)
            for s in range(STEPS + 3):
                tail(2 * B - 1, 1, s)
                if s in GATE_STEPS:
                    gate(1, GATE_STEPS.index(s))
            gate(1, B - 1)
            ffn(1)

_INS = ['L0_attn_x', 'L0_attn_W_disp', 'L0_attn_W_val', 'L0_attn_rel_pos_emb', 'L0_attn_W_strain', 'L0_attn_W_pos', 'L0_attn_W_bond', 'L0_attn_W_dmg', 'L0_attn_b_dmg', 'L0_attn_W_dmg_out', 'L0_attn_b_dmg_out', 'L0_attn_W_cproj', 'L0_ffn_rms_w', 'L0_ffn_gate_w', 'L0_ffn_W1', 'L0_ffn_b1', 'L0_ffn_W2', 'L0_ffn_b2']
_OUTS = [((4, 1024, 128), 'float32')]
def kernel(**inputs):
    import numpy as _np
    import concourse.bacc as _bacc
    from concourse import mybir as _mybir
    from concourse.bass_utils import run_bass_kernel_spmd as _run
    nc = _bacc.Bacc("TRN2", target_bir_lowering=False, num_devices=1)
    arrays, args = {}, []
    for name in _INS:
        a = _np.ascontiguousarray(inputs[name])
        arrays[f"in_{name}_dram"] = a
        args.append(nc.dram_tensor(f"in_{name}_dram", a.shape, _mybir.dt.from_np(a.dtype), kind="ExternalInput").ap())
    for i, (shape, dtype) in enumerate(_OUTS):
        dt = _mybir.dt.from_np(_np.dtype(dtype))
        args.append(nc.dram_tensor(f"out_{i}_dram", shape, dt, kind="ExternalOutput").ap())
    prog(nc, *args)
    r = _run(nc, [arrays], core_ids=[0])
    got = tuple(r.results[0][f"out_{i}_dram"] for i in range(len(_OUTS)))
    return got[0]
```
